# Optimizing a Trainium2 kernel written in Bass

```python
import numpy as np
import jax
import jax.numpy as jnp

def _softmax(x, axis=-1):
    return jax.nn.softmax(x, axis=axis)

def _gelu(x):
    return jax.nn.gelu(x, approximate=True)

def _silu(x):
    return jax.nn.silu(x)

def _sigmoid(x):
    return jax.nn.sigmoid(x)

def _layernorm(x, axis=-1, eps=1e-05):
    m = jnp.mean(x, axis=axis, keepdims=True)
    v = jnp.var(x, axis=axis, keepdims=True)
    return (x - m) / jnp.sqrt(v + eps)

def _scatter_add(tgt, idx, src, axis=0):
    return tgt.at[idx].add(src)

def _segment_sum(src, seg, n):
    return jax.ops.segment_sum(src, seg, n)
kernel_name = 'mk_adaln_d1_jaxref_r8_b50e1b'

def setup_inputs(seed: int=0):
    np.random.seed(seed)
    _w = jnp.asarray

    def _L0_attn_setup():
        import jax, jax.numpy as jnp
        import numpy as np
        import math
        EPS_LN = 1e-05
        SCALE = 16.0

        def layer_norm(x, g):
            mean = jnp.mean(x, axis=-1, keepdims=True)
            var = jnp.var(x, axis=-1, keepdims=True)
            return (x - mean) * jax.lax.rsqrt(var + EPS_LN) * g

        def l2norm(t):
            n = jnp.linalg.norm(t, axis=-1, keepdims=True)
            return t / jnp.maximum(n, 1e-12)
        key = jax.random.key(seed)
        ks = jax.random.split(key, 4)
        b, n, dim, h, dh = (4, 256, 128, 8, 64)
        inner = h * dh
        x = jax.random.normal(ks[0], (b, n, dim), dtype=jnp.float32)
        Wq = jax.random.normal(ks[1], (dim, inner), dtype=jnp.float32) * dim ** (-0.5)
        Wkv = jax.random.normal(ks[2], (dim, 2 * dh), dtype=jnp.float32) * dim ** (-0.5)
        Wout = jax.random.normal(ks[3], (inner, dim), dtype=jnp.float32) * inner ** (-0.5)
        norm_g = jnp.ones((dim,), dtype=jnp.float32)
        out_norm_g = jnp.ones((dim,), dtype=jnp.float32)
        return {'x': x, 'norm_g': norm_g, 'Wq': Wq, 'Wkv': Wkv, 'Wout': Wout, 'out_norm_g': out_norm_g}
    _L0_attn_in = _L0_attn_setup()

    def _L0_ffn_setup():
        import jax, jax.numpy as jnp
        import numpy as np
        B, T, D, E = (4, 128, 128, 8)
        HD = 4 * D
        key = jax.random.key(seed)
        k1, k2, k3, k4 = jax.random.split(key, 4)
        std = 0.5 * D ** (-0.5)
        bound = 3.0 ** 0.5 * std
        x = jax.random.normal(k1, (B, T, D), dtype=jnp.float32)
        router_w = jax.random.normal(k2, (E, D), dtype=jnp.float32) * 0.02
        expert_fc = jax.random.uniform(k3, (E, D, HD), dtype=jnp.float32, minval=-bound, maxval=bound)
        expert_proj = jax.random.normal(k4, (E, D, HD), dtype=jnp.float32) * 0.02
        return {'x': x, 'router_w': router_w, 'expert_fc': expert_fc, 'expert_proj': expert_proj}
    _L0_ffn_in = _L0_ffn_setup()
    _L0_c = _w((lambda *s: np.random.randn(*s).astype(np.float32) * 0.05)(8, 128))
    _L0_wmod = _w((lambda *s: np.random.randn(*s).astype(np.float32) * 0.05)(128, 6 * 128) * 128 ** (-0.5))
    _d = {'L0_attn_x': _L0_attn_in['x'], 'L0_attn_norm_g': _L0_attn_in['norm_g'], 'L0_attn_Wq': _L0_attn_in['Wq'], 'L0_attn_Wkv': _L0_attn_in['Wkv'], 'L0_attn_Wout': _L0_attn_in['Wout'], 'L0_attn_out_norm_g': _L0_attn_in['out_norm_g'], 'L0_ffn_router_w': _L0_ffn_in['router_w'], 'L0_ffn_expert_fc': _L0_ffn_in['expert_fc'], 'L0_ffn_expert_proj': _L0_ffn_in['expert_proj'], 'L0_c': _L0_c, 'L0_wmod': _L0_wmod}
    _x0 = _d['L0_attn_x']
    _d['L0_attn_x'] = jax.random.normal(jax.random.fold_in(jax.random.key(seed), 1), (8, 1024, 128), dtype=_x0.dtype)
    del _x0
    return _d

def reference(L0_attn_x, L0_attn_norm_g, L0_attn_Wq, L0_attn_Wkv, L0_attn_Wout, L0_attn_out_norm_g, L0_ffn_router_w, L0_ffn_expert_fc, L0_ffn_expert_proj, L0_c, L0_wmod):

    def _L0_attn_ref(x, norm_g, Wq, Wkv, Wout, out_norm_g):
        import jax, jax.numpy as jnp
        import numpy as np
        import math
        EPS_LN = 1e-05
        SCALE = 16.0

        def layer_norm(x, g):
            mean = jnp.mean(x, axis=-1, keepdims=True)
            var = jnp.var(x, axis=-1, keepdims=True)
            return (x - mean) * jax.lax.rsqrt(var + EPS_LN) * g

        def l2norm(t):
            n = jnp.linalg.norm(t, axis=-1, keepdims=True)
            return t / jnp.maximum(n, 1e-12)
        b, n, dim = x.shape
        h = 8
        dh = Wkv.shape[-1] // 2
        xn = layer_norm(x, norm_g)
        q = xn @ Wq
        kv = xn @ Wkv
        k, v = (kv[..., :dh], kv[..., dh:])
        q = q.reshape(b, n, h, dh).transpose(0, 2, 1, 3)
        q = q * SCALE
        q = l2norm(q)
        k = l2norm(k)
        rs = math.sqrt(SCALE)
        q = q * rs
        k = k * rs
        sim = jnp.einsum('bhid,bjd->bhij', q, k)
        attn = jax.nn.softmax(sim.astype(jnp.float32), axis=-1).astype(sim.dtype)
        out = jnp.einsum('bhij,bjd->bhid', attn, v)
        out = out.transpose(0, 2, 1, 3).reshape(b, n, h * dh)
        out = out @ Wout
        return layer_norm(out, out_norm_g)

    def _L0_ffn_ref(x, router_w, expert_fc, expert_proj):
        import jax, jax.numpy as jnp
        import numpy as np
        B, T, D, E = (4, 128, 128, 8)
        HD = 4 * D
        logits = jnp.einsum('btd,ed->bte', x, router_w)
        probs = jax.nn.softmax(logits, axis=-1)
        expert_ids = jnp.argmax(probs, axis=-1)
        mask = jax.nn.one_hot(expert_ids, E, dtype=x.dtype)
        h = jnp.einsum('btd,edh->ebth', x, expert_fc)
        h = jnp.square(jax.nn.relu(h))
        out_e = jnp.einsum('ebth,edh->ebtd', h, expert_proj)
        output = jnp.einsum('ebtd,bte->btd', out_e, mask)
        return output
    x = L0_attn_x
    mod = (_silu(L0_c) @ L0_wmod).reshape(L0_c.shape[0], 6, 1, -1)
    sa, ca, ga, sb, cb, gb = (mod[:, 0], mod[:, 1], mod[:, 2], mod[:, 3], mod[:, 4], mod[:, 5])
    ga = (2 * (ga >= 0) - 1) * jnp.maximum(jnp.abs(ga), 0.25)
    gb = (2 * (gb >= 0) - 1) * jnp.maximum(jnp.abs(gb), 0.25)
    h = _layernorm(x, axis=-1) * (1 + ca) + sa
    x = x + ga * _L0_attn_ref(h, L0_attn_norm_g, L0_attn_Wq, L0_attn_Wkv, L0_attn_Wout, L0_attn_out_norm_g)
    h = _layernorm(x, axis=-1) * (1 + cb) + sb
    x = x + gb * _L0_ffn_ref(h, L0_ffn_router_w, L0_ffn_expert_fc, L0_ffn_expert_proj)
    return x

_drawn_inputs = setup_inputs


def setup_inputs(seed=0):
    import zlib

    import numpy as np

    out = dict(_drawn_inputs(seed))
    spreads = {'L0_attn_norm_g': (1.0, 0.2), 'L0_attn_out_norm_g': (1.0, 0.2)}
    factors = {}
    for name, (base, spread) in spreads.items():
        noise = np.random.default_rng([zlib.crc32(name.encode()), seed]).standard_normal(out[name].shape)
        drawn = base * np.exp(spread * noise) if base else spread * noise
        out[name] = jnp.asarray(drawn.astype(out[name].dtype))
    for name, factor in factors.items():
        out[name] = (out[name] * factor).astype(out[name].dtype)
    return out
```

```python
from contextlib import ExitStack

import concourse.bass as bass
from concourse import mybir

F32 = mybir.dt.float32
F16 = mybir.dt.float16
BF16 = mybir.dt.bfloat16
ALU = mybir.AluOpType
ACT = mybir.ActivationFunctionType
AX_X = mybir.AxisListType.X

P = 128
EPS = 1e-5
SCALE = 16.0
LOOK = 2
RING = 4


def build(nc, x, norm_g, wq, wkv, wout, out_g, router, fc, proj, c, wmod, out):
    NB, N, D = x.shape
    H = 8
    INNER = wq.shape[1]
    DH = INNER // H
    E, _, HID = fc.shape
    TB = N // P
    NT = NB * TB
    HT = TB // 2
    HALF = HT * P
    NQK = H + 1
    VC = 2 * DH + 1
    VP = VC + 1
    HC = HID // P
    NS = 8
    assert D == P and DH == 64 and N == 1024 and TB == 8 and 2 * DH == P

    x_t = x.rearrange("b (t p) d -> (b t) p d", p=P)
    out_t = out.rearrange("b (t p) d -> (b t) p d", p=P)
    x1_dram = nc.dram_tensor("x1_scratch", (NT, P, D), F32, kind="Internal").ap()
    h2T_dram = nc.dram_tensor("h2T_scratch", (NT, P, P), F32, kind="Internal").ap()
    lg_dram = nc.dram_tensor("logits_scratch", (NT, P, E), F32, kind="Internal").ap()

    with ExitStack() as ctx:
        def sb(name, shape, dt=F32):
            return ctx.enter_context(nc.sbuf_tensor(name, shape, dt))

        def pb(name, shape, dt=F32):
            return ctx.enter_context(nc.psum_tensor(name, shape, dt))

        sems = []

        def sem(name):
            s = ctx.enter_context(nc.semaphore(name))
            sems.append(s)
            return s

        wq_sb = sb("wq_sb", [P, INNER])
        wkv_sb = sb("wkv_sb", [P, 2 * DH])
        wout_sb = sb("wout_sb", [P, INNER // P, D])
        router_sb = sb("router_sb", [E, D])
        routerT = sb("routerT", [P, E])
        g_col = sb("g_col", [P, 1])
        outg_row = sb("outg_row", [P, D])
        c_T = sb("c_T", [P, NB])
        silu_T = sb("silu_T", [P, NB])
        silu_b = sb("silu_b", [P, NB, P])
        wmod_sb = sb("wmod_sb", [P, 6 * D])
        mod = sb("mod", [P, NB, 6, D])
        gmag = sb("gmag", [P, NB, 2, D])
        ident = sb("ident", [P, P])
        ident16 = sb("ident16", [P, P], F16)
        tick = sb("tick", [P, 1])
        power = sb("power", [P, 16])
        clamp = sb("clamp", [P, NQK])
        rows_a = sb("rows_a", [P, 2, D])
        rows_f = sb("rows_f", [P, 3, D])
        x_in = sb("x_in", [P, D])
        st_a = sb("st_a", [P, 6])
        mv_a = sb("mv_a", [P, 2])
        ve_a = sb("ve_a", [P, 1])
        rs_a = sb("rs_a", [P, 1])
        xn_a = sb("xn_a", [P, D])
        hs_a = sb("hs_a", [P, D])
        h_a = sb("h_a", [P, D])
        st_b = sb("st_b", [P, 6])
        mv_b = sb("mv_b", [P, 2])
        ve_b = sb("ve_b", [P, 1])
        rs_b = sb("rs_b", [P, 1])
        xhat = sb("xhat", [P, D])
        xnT = sb("xnT", [P, P])
        qkv = sb("qkv", [P, INNER + 2 * DH])
        sq = sb("sq", [P, NQK * DH])
        ss = sb("ss", [P, NQK])
        z = sb("z", [P, NQK])
        rq = sb("rq", [P, NQK])
        qn = sb("qn", [P, NQK * DH])
        qs = sb("qs", [P, NQK + 1, 2 * DH], F16)
        q_next = sb("q_next", [P, H, HALF], F16)
        q_cur = sb("q_cur", [P, 2, H, HALF], F16)
        k_next = sb("k_next", [P, 2, N], F16)
        k_cur = sb("k_cur", [P, 2, N], F16)
        v_next = sb("v_next", [P, TB, VP], BF16)
        v_cur = sb("v_cur", [P, TB, VP], BF16)
        probs = sb("probs", [P, RING, 2 * HALF])
        rest = sb("rest", [P, RING, 2 * HALF], BF16)
        o_raw = sb("o_raw", [P, 2, HT, VC])
        o_rin = sb("o_rin", [P, 2, HT])
        o_sum = sb("o_sum", [P, HT, DH])
        o_all = sb("o_all", [P, 2, HT, INNER])
        oT = sb("oT", [P, INNER // P, P])
        y_o = sb("y_o", [P, D])
        x_res = sb("x_res", [P, D])
        st_c = sb("st_c", [P, 6])
        mv_c = sb("mv_c", [P, 2])
        ve_c = sb("ve_c", [P, 1])
        rs_c = sb("rs_c", [P, 1])
        yn = sb("yn", [P, D])
        yg = sb("yg", [P, D])
        x1 = sb("x1", [P, D])
        st_d = sb("st_d", [P, 6])
        mv_d = sb("mv_d", [P, 2])
        ve_d = sb("ve_d", [P, 1])
        rs_d = sb("rs_d", [P, 1])
        hn = sb("hn", [P, D])
        hc = sb("hc", [P, D])
        h2 = sb("h2", [P, D])
        h2T = sb("h2T", [P, P])
        lg = sb("lg", [P, E])

        ps_s = pb("ps_s", [P, 2, 2, HALF])
        ps_o = pb("ps_o", [P, 2, 512])
        ps_m0 = pb("ps_m0", [P, 512])
        ps_m1 = pb("ps_m1", [P, 512])
        ps_m0h = ps_m0[:].bitcast(F16)
        ps_m1h = ps_m1[:].bitcast(F16)

        s_w = sem("weights_loaded")
        s_id = sem("identity_steps")
        s_const = sem("constants_ready")
        s_silu = sem("silu_steps")
        s_silub = sem("silu_broadcast")
        s_modmm = sem("mod_products")
        s_modcp = sem("mod_copied")
        s_modf = sem("mod_finishing")
        s_modr = sem("mod_ready")
        s_rT = sem("router_transposed")
        s_rowa = sem("rows_a_moved")
        s_rowf = sem("rows_f_moved")
        s_tick = sem("waited")
        s_xin = sem("x_in_loaded")
        s_xres = sem("x_res_loaded")
        s_scores = sem("scores_ready")
        s_exp = sem("exp_done")
        s_rest = sem("rest_ready")
        s_pv = sem("pv_done")
        s_ocp = sem("o_copied")
        s_orin = sem("o_reciprocal")
        s_osum = sem("o_summed")
        s_onorm = sem("o_normed")
        s_kst = sem("k_staged")
        s_vst = sem("v_staged")
        s_qst = sem("q_staged")
        s_kcur = sem("k_moved")
        s_vcur = sem("v_moved")
        s_qcur = sem("q_moved")
        s_ones = sem("ones_set")
        s_ja = sem("xhat_transposed")
        s_xnT = sem("xnT_ready")
        s_jq = sem("q_projected")
        s_jkv = sem("kv_projected")
        s_qcp = sem("q_copied")
        s_kvcp = sem("kv_copied")
        s_jqT = sem("q_transposed")
        s_jkT = sem("k_transposed")
        s_jo = sem("o_transposed")
        s_oT = sem("oT_ready")
        s_jy = sem("y_projected")
        s_y = sem("y_copied")
        s_jh = sem("h2_transposed")
        s_h2T = sem("h2T_ready")
        s_jl = sem("logits_product")
        s_lg = sem("logits_copied")
        s_va = sem("var_a")
        s_ra = sem("rsqrt_a")
        s_xa = sem("xn_a_ready")
        s_ha = sem("h_a_steps")
        s_vb = sem("var_b")
        s_rb = sem("rsqrt_b")
        s_xh = sem("xhat_ready")
        s_sq = sem("squares_ready")
        s_ss = sem("norms_squared")
        s_rq = sem("rsqrt_q")
        s_qn = sem("qn_ready")
        s_hi = sem("q_hi_ready")
        s_vhi = sem("v_hi_ready")
        s_lo = sem("q_lo_ready")
        s_vc = sem("var_c")
        s_rc = sem("rsqrt_c")
        s_yn = sem("yn_ready")
        s_x1 = sem("x1_steps")
        s_vd = sem("var_d")
        s_rd = sem("rsqrt_d")
        s_hn = sem("hn_ready")
        s_h2 = sem("h2_steps")
        s_x1o = sem("x1_stored")
        s_h2o = sem("h2T_stored")
        s_lgo = sem("logits_stored")

        def wait(eng, s, v):
            if not isinstance(v, int) or v > 0:
                eng.wait_ge(s, v)

        def known(v, lo, hi):
            return not isinstance(v, int) or lo <= v < hi

        def sweep(eng, macro):
            for m in range(TB):
                macro(-1, m)
            for m in range(TB):
                macro(0, m)
            with eng.Fori(1, NB - 1) as b:
                for m in range(TB):
                    macro(b, m)
            for m in range(TB):
                macro(NB - 1, m)
            for m in range(HT + 2):
                macro(NB, m)

        def rows_of(b, k0, k1, off=0):
            if isinstance(b, int):
                return mod[:, (b + off) % NB, k0:k1, :]
            return mod[:, bass.ds((b + off) % NB if off else b, 1), k0:k1, :].rearrange("p o k d -> p (o k) d")

        def tile_of(ap, b, k):
            if isinstance(b, int):
                return ap[TB * b + k]
            return ap[bass.ds(b * TB + k, 1)].rearrange("o p d -> (o p) d")

        block = ctx.enter_context(nc.Block())

        @block.sync
        def _(sp):
            loads = [
                (wmod_sb[:], wmod), (c_T[:], c),
                (g_col[:], norm_g.rearrange("(d o) -> d o", o=1)),
                (wq_sb[:], wq), (wkv_sb[:], wkv),
                (wout_sb[:], wout.rearrange("(j p) n -> p j n", p=P)),
                (router_sb[:], router),
                (outg_row[:], out_g.rearrange("(o d) -> o d", o=1).broadcast_to([P, D])),
            ]
            sp.dma_start(x_in[:], x_t[0]).then_inc(s_xin, 16)
            for dst, src in loads:
                sp.dma_start(dst, src).then_inc(s_w, 16)

            def macro(b, m):
                M = b * TB + m
                t = M + 9
                if known(t, 1, NT):
                    wait(sp, s_xa, t)
                    if isinstance(b, int):
                        src = x_t[t]
                    elif m == TB - 1:
                        src = x_t[bass.ds(((b + 2) % NB) * TB, 1)].rearrange("o p d -> (o p) d")
                    else:
                        src = tile_of(x_t, b, m + 9)
                    sp.dma_start(x_in[:], src).then_inc(s_xin, 16)
                r = M - 4
                if known(r, 0, NT):
                    wait(sp, s_x1, 2 * r)
                    sp.dma_start(x_res[:], tile_of(x_t, b, m - 4)).then_inc(s_xres, 16)
                r = M - 5
                if known(r, 0, NT):
                    wait(sp, s_x1, 2 * (r + 1))
                    sp.dma_start(tile_of(x1_dram, b, m - 5), x1[:]).then_inc(s_x1o, 16)
                    wait(sp, s_h2T, r + 1)
                    sp.dma_start(tile_of(h2T_dram, b, m - 5), h2T[:]).then_inc(s_h2o, 16)
                    wait(sp, s_lg, r + 1)
                    sp.dma_start(tile_of(lg_dram, b, m - 5), lg[:]).then_inc(s_lgo, 16)

            sweep(sp, macro)
            sp.wait_ge(s_x1o, 16 * NT)
            sp.wait_ge(s_h2o, 16 * NT)
            sp.wait_ge(s_lgo, 16 * NT)

        @block.gpsimd
        def _(pool):
            g = nc.gpsimd
            g.memset(ident[:], 0.0).then_inc(s_id, 1)
            g.memset(power[:], -0.5)
            g.memset(clamp[:, 0:H], 1e-24 / SCALE ** 2 / 16.0)
            g.memset(clamp[:, H:NQK], 1e-24 / 16.0).then_inc(s_id, 1)
            pool.wait_ge(s_id, 2)
            g.affine_select(out=ident[:], in_=ident[:], compare_op=ALU.not_equal, fill=1.0, base=0,
                            pattern=[[-1, P]], channel_multiplier=1).then_inc(s_id, 1)
            pool.wait_ge(s_id, 3)
            g.tensor_copy(ident16[:], ident[:]).then_inc(s_const, 1)
            g.memset(v_next[:], 1.0).then_inc(s_ones, 1)
            g.memset(v_cur[:], 1.0).then_inc(s_ones, 1)
            pool.wait_ge(s_ones, 2)
            pool.wait_ge(s_modr, 1)

            def macro(b, m):
                M = b * TB + m
                ta, t, r, rp = M + 9, M + 8, M - 4, M - 5
                def rsqrt(dst, src, have, done, n):
                    wait(pool, have, n)
                    g.tensor_tensor(dst, src, power[:, 0:src.shape[1]], ALU.pow).then_inc(done, 1)

                def norm_o(u, free):
                    wait(pool, s_ocp, u + 1)
                    wait(pool, s_onorm, u)
                    raw = o_raw[:, um, :, :]
                    g.tensor_tensor(o_sum[:], raw[:, :, 0:DH], raw[:, :, DH:2 * DH], ALU.add).then_inc(s_osum, 1)
                    wait(pool, s_osum, u + 1)
                    wait(pool, s_orin, u + 1)
                    if free is not None:
                        wait(pool, s_jo, free)
                    g.tensor_tensor(o_all[:, uh, :, hh * DH:(hh + 1) * DH], o_sum[:],
                                    o_rin[:, um, :].rearrange("p (t o) -> p t o", o=1).broadcast_to([P, HT, DH]),
                                    ALU.mult).then_inc(s_onorm, 1)

                if known(M - 1, 0, NT):
                    mm = (m - 1) % TB
                    um, uh, hh = 1, mm // 4, 2 * (mm % 4) + 1
                    norm_o(2 * M - 1, None)
                if known(ta, 0, NT):
                    rsqrt(rs_a[:], ve_a[:], s_va, s_ra, 3 * (ta + 1))
                if known(rp, 0, NT):
                    rsqrt(rs_c[:], ve_c[:], s_vc, s_rc, 3 * (rp + 1))
                if known(ta, 0, NT):
                    wait(pool, s_xa, ta + 1)
                    if m == TB - 1:
                        wait(pool, s_rowa, b + 3)
                    g.tensor_tensor(hs_a[:], xn_a[:], rows_a[:, 1, :], ALU.mult).then_inc(s_ha, 1)
                    wait(pool, s_ha, 2 * ta + 1)
                    g.tensor_tensor(h_a[:], hs_a[:], rows_a[:, 0, :], ALU.add).then_inc(s_ha, 1)
                if known(rp, 0, NT):
                    wait(pool, s_yn, rp + 1)
                    if m == 5:
                        wait(pool, s_rowf, b + 1)
                    g.tensor_tensor(yg[:], yn[:], rows_f[:, 0, :], ALU.mult).then_inc(s_x1, 1)
                    wait(pool, s_x1, 2 * rp + 1)
                    wait(pool, s_xres, 16 * (rp + 1))
                    wait(pool, s_x1o, 16 * rp)
                    g.tensor_tensor(x1[:], yg[:], x_res[:], ALU.add).then_inc(s_x1, 1)
                if known(ta, 0, NT):
                    rsqrt(rs_b[:], ve_b[:], s_vb, s_rb, 3 * (ta + 1))
                if known(rp, 0, NT):
                    rsqrt(rs_d[:], ve_d[:], s_vd, s_rd, 3 * (rp + 1))
                if known(t, 0, NT):
                    wait(pool, s_qcp, t + 1)
                    wait(pool, s_kvcp, t + 1)
                    g.tensor_tensor(sq[:], qkv[:, 0:NQK * DH], qkv[:, 0:NQK * DH], ALU.mult).then_inc(s_sq, 1)
                if known(rp, 0, NT):
                    wait(pool, s_hn, rp + 1)
                    g.tensor_tensor(hc[:], hn[:], rows_f[:, 2, :], ALU.mult).then_inc(s_h2, 1)
                    wait(pool, s_h2, 2 * rp + 1)
                    wait(pool, s_jh, rp)
                    g.tensor_tensor(h2[:], hc[:], rows_f[:, 1, :], ALU.add).then_inc(s_h2, 1)
                if known(M, 0, NT):
                    um, uh, hh = 0, m // 4, 2 * (m % 4)
                    norm_o(2 * M, 4 * (M // 4 - 1) if isinstance(b, int) and m % 4 == 0
                           else (8 * b + 4 * (m // 4 - 1) if m % 4 == 0 else None))
                if known(t, 0, NT):
                    rsqrt(rq[:], z[:], s_ss, s_rq, 2 * (t + 1))

            pool.wait_ge(s_va, 3)
            g.tensor_tensor(rs_a[:], ve_a[:], power[:, 0:1], ALU.pow).then_inc(s_ra, 1)
            pool.wait_ge(s_xa, 1)
            pool.wait_ge(s_rowa, 1)
            g.tensor_tensor(hs_a[:], xn_a[:], rows_a[:, 1, :], ALU.mult).then_inc(s_ha, 1)
            pool.wait_ge(s_ha, 1)
            g.tensor_tensor(h_a[:], hs_a[:], rows_a[:, 0, :], ALU.add).then_inc(s_ha, 1)
            pool.wait_ge(s_vb, 3)
            g.tensor_tensor(rs_b[:], ve_b[:], power[:, 0:1], ALU.pow).then_inc(s_rb, 1)
            sweep(pool, macro)

        @block.scalar
        def _(act):
            a = nc.scalar
            act.wait_ge(s_w, 16 * 8)
            a.activation(silu_T[:], c_T[:], ACT.Exp, scale=-1.0).then_inc(s_silu, 1)
            for b in range(NB):
                act.wait_ge(s_modmm, b + 1)
                a.copy(mod[:, b, 0:3, :], ps_s[:, b % 2, 0, 0:3 * D].rearrange("p (k d) -> p k d", k=3))
                a.copy(mod[:, b, 3:6, :], ps_s[:, b % 2, 1, 0:3 * D].rearrange("p (k d) -> p k d", k=3)
                       ).then_inc(s_modcp, 1)
            act.wait_ge(s_rT, 1)
            a.copy(routerT[:], ps_m0[:, 0:E]).then_inc(s_modcp, 1)

            def macro(b, m):
                M = b * TB + m
                t, tp, r, rp = M + 8, M + 7, M - 4, M - 5
                for s in range(NS):
                    X = M * NS + s
                    if s in (0, 4):
                        U = 2 * M - 1 if s == 0 else 2 * M
                        if known(M - (s == 0), 0, NT):
                            wait(act, s_pv, 4 * (U + 1))
                            wait(act, s_onorm, U - 1)
                            par = 1 if s == 0 else 0
                            a.copy(o_raw[:, par, :, :].rearrange("p (k t) d -> p k (t d)", k=2),
                                   ps_o[:, :, 0:2 * VC]).then_inc(s_ocp, 1)
                    if s == 0 and known(tp, 0, NT):
                        qm = (m - 1) % TB
                        wait(act, s_jqT, tp + 1)
                        wait(act, s_qcur, 2 * b + 1 + (1 if m > 4 else 0) if m > 0 else 2 * b)
                        a.copy(q_next[:, :, (qm % HT) * P:(qm % HT + 1) * P],
                               ps_m0h[:, 0:H * P].rearrange("p (h n) -> p h n", h=H)).then_inc(s_qst, 1)
                        wait(act, s_jkT, tp + 1)
                        wait(act, s_kcur, 4 * b + qm // 2 + 1 if m > 0 else 4 * (b - 1) + qm // 2 + 1)
                        a.copy(k_next[:, :, qm * P:(qm + 1) * P],
                               ps_m1h[:, 0:2 * P].rearrange("p (h n) -> p h n", h=2)).then_inc(s_kst, 1)
                    if s == 1 and known(t, 0, NT):
                        wait(act, s_ja, t + 1)
                        wait(act, s_jkv, t)
                        a.activation(xnT[:], ps_m0[:, 0:P], ACT.Copy, scale=g_col[:, 0:1]).then_inc(s_xnT, 1)
                    if s == 3 and known(t, 0, NT):
                        wait(act, s_jq, t + 1)
                        wait(act, s_qn, t)
                        a.copy(qkv[:, 0:INNER], ps_m0[:, 0:INNER]).then_inc(s_qcp, 1)
                        wait(act, s_jkv, t + 1)
                        wait(act, s_vst, t)
                        a.copy(qkv[:, INNER:INNER + 2 * DH], ps_m1[:, 0:2 * DH]).then_inc(s_kvcp, 1)
                    if s == 4 and known(r, 0, NT):
                        wait(act, s_jo, r + 1)
                        wait(act, s_jy, r)
                        a.copy(oT[:], ps_m1[:].rearrange("p (j n) -> p j n", n=P)).then_inc(s_oT, 1)
                    if s == 6 and known(r, 0, NT):
                        wait(act, s_jy, r + 1)
                        wait(act, s_yn, r)
                        a.copy(y_o[:], ps_m0[:, 0:D]).then_inc(s_y, 1)
                    if s == 5 and known(rp, 0, NT):
                        wait(act, s_jh, rp + 1)
                        wait(act, s_jl, rp)
                        wait(act, s_h2o, 16 * rp)
                        a.copy(h2T[:], ps_m1[:, 0:P]).then_inc(s_h2T, 1)
                    if s == 7 and known(rp, 0, NT):
                        wait(act, s_jl, rp + 1)
                        wait(act, s_lgo, 16 * rp)
                        a.copy(lg[:], ps_m0[:, 0:E]).then_inc(s_lg, 1)
                    if known(X + LOOK, 0, NT * NS):
                        k = (s + LOOK) % NS
                        wait(act, s_scores, X + LOOK + 1)
                        wait(act, s_pv, X + LOOK - RING + 1)
                        a.activation(probs[:, k % RING, :], ps_s[:, k % 2, :, :].rearrange("p k n -> p (k n)"),
                                     ACT.Exp).then_inc(s_exp, 1)

            sweep(act, macro)

        @block.vector
        def _(dve):
            v = nc.vector
            dve.wait_ge(s_silu, 1)
            v.tensor_scalar_add(silu_T[:], silu_T[:], 1.0).then_inc(s_silu, 1)
            dve.wait_ge(s_silu, 2)
            v.reciprocal(silu_T[:], silu_T[:]).then_inc(s_silu, 1)
            dve.wait_ge(s_silu, 3)
            v.tensor_tensor(silu_T[:], silu_T[:], c_T[:], ALU.mult).then_inc(s_silu, 1)
            dve.wait_ge(s_silu, 4)
            v.tensor_copy(silu_b[:], silu_T[:].rearrange("p (b o) -> p b o", o=1).broadcast_to([P, NB, P])
                          ).then_inc(s_silub, 1)
            dve.wait_ge(s_modcp, NB)
            n = [0]

            def link(ins):
                n[0] += 1
                ins.then_inc(s_modf, 1)
                dve.wait_ge(s_modf, n[0])
            link(v.tensor_scalar_add(mod[:, :, 1, :], mod[:, :, 1, :], 1.0))
            link(v.tensor_scalar_add(mod[:, :, 4, :], mod[:, :, 4, :], 1.0))
            for j, k in ((0, 2), (1, 5)):
                link(v.tensor_scalar(gmag[:, :, 0, :], mod[:, :, k, :], -1.0, 0.25, ALU.mult, ALU.max))
                link(v.tensor_tensor(gmag[:, :, 0, :], gmag[:, :, 0, :], mod[:, :, k, :], ALU.max))
                link(v.tensor_scalar(gmag[:, :, 1, :], mod[:, :, k, :], 0.0, 2.0, ALU.is_ge, ALU.mult))
                link(v.tensor_scalar_add(gmag[:, :, 1, :], gmag[:, :, 1, :], -1.0))
                link(v.tensor_tensor(mod[:, :, k, :], gmag[:, :, 0, :], gmag[:, :, 1, :], ALU.mult))
            v.tensor_tensor(mod[:, :, 2, :], mod[:, :, 2, :],
                            outg_row[:].rearrange("p (o d) -> p o d", o=1).broadcast_to([P, NB, D]),
                            ALU.mult).then_inc(s_modr, 1)

            def stats(src, st, mv, ve, chain, i):
                v.bn_stats(st[:], src[:]).then_inc(chain, 1)
                wait(dve, chain, 3 * i + 1)
                v.tensor_scalar_add(tick[:], power[:, 0:1], 1.0)
                v.bn_aggr(mv[:], st[:]).then_inc(chain, 1)
                wait(dve, chain, 3 * i + 2)
                v.tensor_scalar_add(ve[:], mv[:, 1:2], EPS).then_inc(chain, 1)

            def normed(dst, src, mv, rs, done):
                v.tensor_scalar(dst[:], src[:], mv[:, 0:1], rs[:, 0:1], ALU.subtract, ALU.mult).then_inc(done, 1)

            def a_stats(i):
                wait(dve, s_xin, 16 * (i + 1))
                stats(x_in, st_a, mv_a, ve_a, s_va, i)

            def a_norm(i):
                wait(dve, s_ra, i + 1)
                wait(dve, s_va, 3 * (i + 1))
                wait(dve, s_ha, 2 * i)
                normed(xn_a, x_in, mv_a, rs_a, s_xa)

            def b_stats(i):
                wait(dve, s_ha, 2 * (i + 1))
                stats(h_a, st_b, mv_b, ve_b, s_vb, i)

            def b_norm(i):
                wait(dve, s_rb, i + 1)
                wait(dve, s_vb, 3 * (i + 1))
                wait(dve, s_ja, i)
                normed(xhat, h_a, mv_b, rs_b, s_xh)

            dve.wait_ge(s_const, 1)
            dve.wait_ge(s_modr, 1)
            v.tensor_scalar(rows_a[:], rows_of(0, 0, 2), 1.0, None, ALU.mult).then_inc(s_rowa, 1)
            a_stats(0)
            a_norm(0)
            b_stats(0)
            b_norm(0)

            def macro(b, m):
                M = b * TB + m
                ta, t, r, rp = M + 9, M + 8, M - 4, M - 5
                for s in range(NS):
                    X = M * NS + s
                    if m == 0 and s < 4 and known(b, 0, NB):
                        wait(dve, s_vst, TB * b + 2 * s + 2)
                        wait(dve, s_pv, (b - 1) * TB * NS + TB * NS - 3 + s)
                        wait(dve, s_ones, 2)
                        v.tensor_copy(v_cur[:, 2 * s:2 * s + 2, :], v_next[:, 2 * s:2 * s + 2, :]).then_inc(s_vcur, 1)
                    if known(X, 0, NT * NS):
                        wait(dve, s_exp, X + 1)
                        wait(dve, s_pv, X - RING + 1)
                        pr = probs[:, s % RING, :]
                        hi = pr.bitcast(BF16).rearrange("p (n two) -> p n two", two=2)[:, :, 1]
                        v.tensor_tensor(rest[:, s % RING, :], pr, hi, ALU.subtract).then_inc(s_rest, 1)

                    def k_move(bn, j):
                        wait(dve, s_kst, TB * bn + 2 * j + 2)
                        wait(dve, s_scores, (bn - 1) * TB * NS + TB * NS - 3 + j)
                        v.tensor_copy(k_cur[:, :, 2 * j * P:(2 * j + 2) * P],
                                      k_next[:, :, 2 * j * P:(2 * j + 2) * P]).then_inc(s_kcur, 1)

                    def q_move(bn, half):
                        wait(dve, s_qst, TB * bn + HT * (half + 1))
                        wait(dve, s_scores, (bn - 1) * TB * NS + 4 * NS * (half + 1))
                        v.tensor_copy(q_cur[:, half, :, :], q_next[:]).then_inc(s_qcur, 1)

                    if m == TB - 1 and s in (5, 6, 7) and known(b + 1, 0, NB):
                        k_move(b + 1, s - 5)
                    if m == 0 and s == 1 and known(b, 0, NB):
                        k_move(b, 3)
                        q_move(b, 1)
                    if m == 4 and s == 2 and known(b + 1, 0, NB):
                        q_move(b + 1, 0)

                    if s in (1, 5):
                        U = 2 * M - 1 if s == 1 else 2 * M
                        if known(M - (s == 1), 0, NT):
                            par = 1 if s == 1 else 0
                            wait(dve, s_ocp, U + 1)
                            wait(dve, s_onorm, U - 1)
                            v.reciprocal(o_rin[:, par, :], o_raw[:, par, :, 2 * DH]).then_inc(s_orin, 1)
                    if s == 0:
                        if m == TB - 1 and known(ta, 0, NT):
                            wait(dve, s_ha, 2 * ta)
                            v.tensor_scalar(rows_a[:], rows_of(b, 0, 2, 2), 1.0, None, ALU.mult).then_inc(s_rowa, 1)
                        if m == 5 and known(rp, 0, NT):
                            wait(dve, s_h2, 2 * rp)
                            v.tensor_scalar(rows_f[:], rows_of(b, 2, 5), 1.0, None, ALU.mult).then_inc(s_rowf, 1)
                        if known(ta, 0, NT):
                            a_stats(ta)
                        if known(rp, 0, NT):
                            wait(dve, s_y, rp + 1)
                            stats(y_o, st_c, mv_c, ve_c, s_vc, rp)
                    if s == 1:
                        if known(ta, 0, NT):
                            a_norm(ta)
                        if known(rp, 0, NT):
                            wait(dve, s_rc, rp + 1)
                            wait(dve, s_vc, 3 * (rp + 1))
                            wait(dve, s_x1, 2 * rp)
                            normed(yn, y_o, mv_c, rs_c, s_yn)
                    if s == 3:
                        if known(ta, 0, NT):
                            b_stats(ta)
                        if known(rp, 0, NT):
                            wait(dve, s_x1, 2 * (rp + 1))
                            stats(x1, st_d, mv_d, ve_d, s_vd, rp)
                    if s == 4:
                        if known(ta, 0, NT):
                            b_norm(ta)
                        if known(rp, 0, NT):
                            wait(dve, s_rd, rp + 1)
                            wait(dve, s_vd, 3 * (rp + 1))
                            wait(dve, s_h2, 2 * rp)
                            normed(hn, x1, mv_d, rs_d, s_hn)
                    if known(t, 0, NT):
                        qn3 = qn[:].rearrange("p (h d) -> p h d", d=DH)
                        if s == 5:
                            wait(dve, s_sq, t + 1)
                            v.tensor_reduce(ss[:], sq[:].rearrange("p (h d) -> p h d", d=DH), AX_X,
                                            ALU.add).then_inc(s_ss, 1)
                            wait(dve, s_ss, 2 * t + 1)
                            v.scalar_tensor_tensor(out=z[:], in0=ss[:], scalar=1.0 / SCALE, in1=clamp[:],
                                                   op0=ALU.mult, op1=ALU.max).then_inc(s_ss, 1)
                        if s == 6:
                            wait(dve, s_rq, t + 1)
                            wait(dve, s_kvcp, t + 1)
                            v.tensor_tensor(qn3, qkv[:, 0:NQK * DH].rearrange("p (h d) -> p h d", d=DH),
                                            rq[:].rearrange("p (h o) -> p h o", o=1).broadcast_to([P, NQK, DH]),
                                            ALU.mult).then_inc(s_qn, 1)
                            wait(dve, s_jqT, t)
                            wait(dve, s_jkT, t)
                            wait(dve, s_qn, t + 1)
                            v.tensor_copy(qs[:, 0:NQK, 0:DH], qn3)
                            v.tensor_copy(qs[:, H, DH:2 * DH], qn3[:, H, :]).then_inc(s_hi, 1)
                            wait(dve, s_vcur, 4 * b + m // 2 + 1)
                            v.tensor_copy(v_next[:, m, 0:DH], qkv[:, NQK * DH:(NQK + 1) * DH]).then_inc(s_vhi, 1)
                        if s == 7:
                            wait(dve, s_hi, t + 1)
                            v.tensor_tensor(qs[:, 0:H, DH:2 * DH], qn3[:, 0:H, :], qs[:, 0:H, 0:DH], ALU.subtract)
                            v.tensor_tensor(qs[:, H + 1, 0:DH], qn3[:, H, :], qs[:, H, 0:DH], ALU.subtract)
                            v.tensor_tensor(qs[:, H + 1, DH:2 * DH], qn3[:, H, :], qs[:, H, 0:DH],
                                            ALU.subtract).then_inc(s_lo, 1)
                            wait(dve, s_vhi, t + 1)
                            v.tensor_tensor(v_next[:, m, DH:2 * DH], qkv[:, NQK * DH:(NQK + 1) * DH],
                                            v_next[:, m, 0:DH], ALU.subtract).then_inc(s_vst, 1)

            sweep(dve, macro)

        @block.tensor
        def _(pe):
            te = nc.tensor
            pe.wait_ge(s_silub, 1)
            for b in range(NB):
                wait(pe, s_modcp, b - 1)
                te.matmul(ps_s[:, b % 2, 0, 0:3 * D], silu_b[:, b, :], wmod_sb[:, 0:3 * D], start=True, stop=True)
                te.matmul(ps_s[:, b % 2, 1, 0:3 * D], silu_b[:, b, :], wmod_sb[:, 3 * D:6 * D],
                          start=True, stop=True).then_inc(s_modmm, 1)
            pe.wait_ge(s_const, 1)
            te.transpose(ps_m0[:, 0:E], router_sb[:], ident[0:E, 0:E]).then_inc(s_rT, 1)
            pe.wait_ge(s_modcp, NB + 1)

            def macro(b, m):
                M = b * TB + m
                t, tp, r, rp = M + 8, M + 7, M - 4, M - 5
                for s in range(NS):
                    X = M * NS + s
                    if s == 0 and known(tp, 0, NT):
                        wait(pe, s_lo, tp + 1)
                        wait(pe, s_lg, rp)
                        if isinstance(b, int):
                            wait(pe, s_y, r)
                        for h in range(H):
                            last = te.transpose(ps_m0h[:, h * P:(h + 1) * P], qs[:, h, :], ident16[:])
                        last.then_inc(s_jqT, 1)
                        wait(pe, s_h2T, rp)
                        if isinstance(b, int):
                            wait(pe, s_oT, r)
                        for j in range(2):
                            last = te.transpose(ps_m1h[:, j * P:(j + 1) * P], qs[:, H + j, :], ident16[:])
                        last.then_inc(s_jkT, 1)
                    if s == 1 and known(t, 0, NT):
                        wait(pe, s_xh, t + 1)
                        wait(pe, s_qst, t)
                        te.transpose(ps_m0[:, 0:P], xhat[:], ident[:]).then_inc(s_ja, 1)
                    if s == 3 and known(t, 0, NT):
                        wait(pe, s_xnT, t + 1)
                        te.matmul(ps_m0[:, 0:INNER], xnT[:], wq_sb[:], start=True, stop=True).then_inc(s_jq, 1)
                        wait(pe, s_kst, t)
                        te.matmul(ps_m1[:, 0:2 * DH], xnT[:], wkv_sb[:], start=True, stop=True).then_inc(s_jkv, 1)
                    if s == 4 and known(r, 0, NT):
                        wait(pe, s_onorm, 8 * (r // 4 + 1) if isinstance(b, int)
                             else 16 * b + 8 * ((m - 4) // 4 + 1))
                        wait(pe, s_kvcp, (t + 1) if not isinstance(t, int) else min(t + 1, NT))
                        g_par = ((m - 4) // 4) % 2
                        for j in range(INNER // P):
                            last = te.transpose(ps_m1[:, j * P:(j + 1) * P], o_all[:, g_par, (m - 4) % 4, j * P:(j + 1) * P],
                                                ident[:])
                        last.then_inc(s_jo, 1)
                    if s == 5 and known(rp, 0, NT):
                        wait(pe, s_h2, 2 * (rp + 1))
                        wait(pe, s_oT, (r + 1) if not isinstance(r, int) else min(r + 1, NT))
                        te.transpose(ps_m1[:, 0:P], h2[:], ident[:]).then_inc(s_jh, 1)
                    if s == 6 and known(r, 0, NT):
                        wait(pe, s_oT, r + 1)
                        wait(pe, s_qcp, (t + 1) if not isinstance(t, int) else min(t + 1, NT))
                        for j in range(INNER // P):
                            last = te.matmul(ps_m0[:, 0:D], oT[:, j, :], wout_sb[:, j, :], start=(j == 0),
                                             stop=(j == INNER // P - 1))
                        last.then_inc(s_jy, 1)
                    if s == 7 and known(rp, 0, NT):
                        wait(pe, s_h2T, rp + 1)
                        wait(pe, s_y, (r + 1) if not isinstance(r, int) else min(r + 1, NT))
                        te.matmul(ps_m0[:, 0:E], h2T[:], routerT[:], start=True, stop=True).then_inc(s_jl, 1)

                    if known(X + LOOK, 0, NT * NS):
                        s2 = s + LOOK
                        m2 = m + s2 // NS
                        s2 %= NS
                        bo, m2 = m2 // TB, m2 % TB
                        half, h, jj = m2 // 4, 2 * (m2 % 4) + s2 // 4, s2 % 4
                        if m2 % 4 == 0 and s2 == 0:
                            wait(pe, s_qcur, 2 * (b + bo) + half + 1)
                        if m2 == 0 and s2 < 4:
                            wait(pe, s_kcur, 4 * (b + bo) + jj + 1)
                        wait(pe, s_exp, X + LOOK - 1)
                        for jc in range(2):
                            for part in range(2):
                                ch = 2 * jj + jc
                                last = te.matmul(ps_s[:, s2 % 2, jc, :], k_cur[:, part, ch * P:(ch + 1) * P],
                                                 q_cur[:, half, h, :], start=(part == 0), stop=(part == 1))
                        last.then_inc(s_scores, 1)
                    if known(X, 0, NT * NS):
                        jj = s % 4
                        if m == 0 and s < 4:
                            wait(pe, s_vcur, 4 * b + jj + 1)
                        if jj == 0:
                            wait(pe, s_ocp, 2 * M + s // 4)
                        wait(pe, s_rest, X + 1)
                        pr = probs[:, s % RING, :]
                        hi = pr.bitcast(BF16).rearrange("p (n two) -> p n two", two=2)[:, :, 1]
                        for jc in range(2):
                            for it in range(HT):
                                o = ps_o[:, it // 2, (it % 2) * VC:(it % 2 + 1) * VC]
                                vv = v_cur[:, 2 * jj + jc, 0:VC]
                                cols = slice(jc * HALF + it * P, jc * HALF + (it + 1) * P)
                                te.matmul(o, hi[:, cols], vv, start=(jj == 0 and jc == 0 and it % 2 == 0),
                                          stop=False, skip_group_check=True)
                                last = te.matmul(o, rest[:, s % RING, cols], vv, start=False,
                                                 stop=(jj == 3 and jc == 1), skip_group_check=True)
                        last.then_inc(s_pv, 1)

            sweep(pe, macro)

    with ExitStack() as ctx:
        build_ffn(nc, ctx, NB, NT, E, D, HID, HC, x1_dram, h2T_dram, lg_dram, fc, proj, c, wmod, out_t)


def build_ffn(nc, ctx, NB, NT, E, D, HID, HC, x1_dram, h2T_dram, lg_dram, fc, proj, c, wmod, out_t):
    def sb(name, shape, dt=F32):
        return ctx.enter_context(nc.sbuf_tensor(name, shape, dt))

    def pb(name, shape, dt=F32):
        return ctx.enter_context(nc.psum_tensor(name, shape, dt))

    def sem(name):
        return ctx.enter_context(nc.semaphore(name))

    G = 4
    NG = NT // G
    fc_sb = sb("fc_sb", [P, E, HID])
    pj_sb = sb("pj_sb", [P, E, HID])
    pjT = sb("pjT", [P, E, HC, D])
    ident2 = sb("ident2", [P, P])
    gbrow = sb("gbrow", [P, NB, D])
    gbm = sb("gbm", [P, NB, 2, D])
    cT2 = sb("cT2", [P, NB])
    sT2 = sb("sT2", [P, NB])
    sb2 = sb("sb2", [P, NB, P])
    wm2 = sb("wm2", [P, D])
    rank = sb("rank", [P, E])
    h2T = sb("f_h2T", [P, G * P])
    x1 = sb("f_x1", [P, G, D])
    lg = sb("f_lg", [P, G, E])
    mx = sb("f_mx", [P, G])
    mk = sb("f_mk", [P, G, E])
    rl = sb("f_rl", [P, 2, G * P])
    hh = sb("f_hh", [P, 2, HC, G * P])
    acc = sb("f_acc", [P, 2, G, D])
    ps_h = pb("ps_h", [P, 4, 512])
    ps_y = pb("ps_y", [P, 2, 512])
    ps_t = pb("ps_t", [P, 2, 512])
    f_w = sem("f_weights")
    f_i = sem("f_ident")
    f_c = sem("f_chain")
    f_t = sem("f_transposed")
    f_tc = sem("f_transposed_copied")
    f_in = sem("f_inputs")
    f_mk = sem("f_mask")
    f_hm = sem("f_h_product")
    f_rl = sem("f_relu")
    f_sq = sem("f_squared")
    f_y = sem("f_y_product")
    f_ac = sem("f_accumulated")
    f_out = sem("f_out")
    f_gm = sem("f_gate_products")
    block = ctx.enter_context(nc.Block())
    HM = E * HC

    @block.sync
    def _(sp):
        sp.dma_start(fc_sb[:], fc.rearrange("e d h -> d e h")).then_inc(f_w, 16)
        sp.dma_start(pj_sb[:], proj.rearrange("e d h -> d e h")).then_inc(f_w, 16)
        sp.dma_start(cT2[:], c).then_inc(f_w, 16)
        sp.dma_start(wm2[:], wmod[:, 5 * D:6 * D]).then_inc(f_w, 16)
        with sp.Fori(0, NG) as i:
            sp.wait_ge(f_ac, i * E)
            sp.wait_ge(f_y, i * E)
            sp.dma_start(h2T[:].rearrange("p (g n) -> p g n", g=G),
                         h2T_dram[bass.ds(i * G, G)].rearrange("g p n -> p g n")).then_inc(f_in, 16)
            sp.wait_ge(f_out, 16 * i)
            sp.dma_start(x1[:], x1_dram[bass.ds(i * G, G)].rearrange("g p n -> p g n")).then_inc(f_in, 16)
            sp.dma_start(lg[:], lg_dram[bass.ds(i * G, G)].rearrange("g p n -> p g n")).then_inc(f_in, 16)
            sp.wait_ge(f_ac, (i + 1) * E + 0)
            sp.wait_ge(f_mk, (i + 1) * 8)
            sp.dma_start(out_t[bass.ds(i * G, G)].rearrange("g p n -> p g n"), acc[:, 1, :, :]).then_inc(f_out, 16)
        sp.wait_ge(f_out, 16 * NG)

    @block.gpsimd
    def _(pool):
        g = nc.gpsimd
        for e in range(E):
            g.memset(rank[:, e:e + 1], float(E - e))
        g.memset(ident2[:], 0.0).then_inc(f_i, 1)
        pool.wait_ge(f_i, 1)
        g.affine_select(out=ident2[:], in_=ident2[:], compare_op=ALU.not_equal, fill=1.0, base=0,
                        pattern=[[-1, P]], channel_multiplier=1).then_inc(f_i, 1)
        with pool.Fori(0, NG) as i:
            for e in range(E):
                for j in range(HC):
                    pool.wait_ge(f_rl, i * HM + (e * HC + j + 1))
                    if e >= 2:
                        pool.wait_ge(f_y, i * E + e - 1)
                    else:
                        pool.wait_ge(f_y, i * E)
                    pool.wait_ge(f_i, 2)
                    k = (e * HC + j) % 2
                    g.tensor_tensor(hh[:, e % 2, j, :], rl[:, k, :], rl[:, k, :], ALU.mult).then_inc(f_sq, 1)

    @block.scalar
    def _(act):
        a = nc.scalar
        act.wait_ge(f_w, 64)
        a.activation(sT2[:], cT2[:], ACT.Exp, scale=-1.0).then_inc(f_c, 1)
        for n in range(E):
            act.wait_ge(f_t, n + 1)
            a.copy(pjT[:, n, :, :], ps_t[:, n % 2, :].rearrange("p (j d) -> p j d", j=HC)).then_inc(f_tc, 1)
        for b in range(NB):
            act.wait_ge(f_gm, b + 1)
            a.copy(gbrow[:, b, :], ps_t[:, b % 2, 0:D]).then_inc(f_tc, 1)
        with act.Fori(0, NG) as i:
            for n in range(HM):
                act.wait_ge(f_hm, i * HM + (n + 1))
                if n >= 2:
                    act.wait_ge(f_sq, i * HM + (n - 1))
                else:
                    act.wait_ge(f_sq, i * HM)
                act.wait_ge(f_w, 64)
                a.activation(rl[:, n % 2, :], ps_h[:, n % 4, :], ACT.Relu).then_inc(f_rl, 1)

    @block.vector
    def _(dve):
        v = nc.vector
        n = [0]

        def link(ins, s=f_c, base=0):
            n[0] += 1
            ins.then_inc(f_c, 1)
            dve.wait_ge(f_c, n[0])
        dve.wait_ge(f_c, 1)
        dve.wait_ge(f_i, 2)
        n[0] = 1
        link(v.tensor_scalar_add(sT2[:], sT2[:], 1.0))
        link(v.reciprocal(sT2[:], sT2[:]))
        link(v.tensor_tensor(sT2[:], sT2[:], cT2[:], ALU.mult))
        link(v.tensor_copy(sb2[:], sT2[:].rearrange("p (b o) -> p b o", o=1).broadcast_to([P, NB, P])))
        dve.wait_ge(f_tc, E + NB)
        link(v.tensor_scalar(gbm[:, :, 0, :], gbrow[:], -1.0, 0.25, ALU.mult, ALU.max))
        link(v.tensor_tensor(gbm[:, :, 0, :], gbm[:, :, 0, :], gbrow[:], ALU.max))
        link(v.tensor_scalar(gbm[:, :, 1, :], gbrow[:], 0.0, 2.0, ALU.is_ge, ALU.mult))
        link(v.tensor_scalar_add(gbm[:, :, 1, :], gbm[:, :, 1, :], -1.0))
        link(v.tensor_tensor(gbrow[:], gbm[:, :, 0, :], gbm[:, :, 1, :], ALU.mult))
        with dve.Fori(0, NG) as i:
            dve.wait_ge(f_in, (i + 1) * 48)
            dve.wait_ge(f_out, i * 16)
            dve.wait_ge(f_w, 64)

            def step(k, ins):
                ins.then_inc(f_mk, 1)
                dve.wait_ge(f_mk, i * 8 + k)
                dve.wait_ge(f_w, 64)
            bro = mx[:].rearrange("p (g o) -> p g o", o=1).broadcast_to([P, G, E])
            step(1, v.tensor_reduce(mx[:], lg[:], AX_X, ALU.max))
            step(2, v.tensor_tensor(mk[:], lg[:], bro, ALU.is_equal))
            step(3, v.tensor_tensor(mk[:], mk[:], rank[:].rearrange("p (o e) -> p o e", o=1).broadcast_to([P, G, E]),
                                    ALU.mult))
            step(4, v.tensor_reduce(mx[:], mk[:], AX_X, ALU.max))
            step(5, v.tensor_tensor(mk[:], mk[:], bro, ALU.is_equal))
            for e in range(E):
                dve.wait_ge(f_y, i * E + (e + 1))
                if e:
                    dve.wait_ge(f_ac, i * E + e)
                dve.wait_ge(f_w, 64)
                for k in range(G):
                    y = ps_y[:, e % 2, k * D:(k + 1) * D]
                    if e == 0:
                        last = v.tensor_scalar(acc[:, 0, k, :], y, mk[:, k, e:e + 1], None, ALU.mult)
                    else:
                        last = v.scalar_tensor_tensor(out=acc[:, 0, k, :], in0=y, scalar=mk[:, k, e:e + 1],
                                                      in1=acc[:, 0, k, :], op0=ALU.mult, op1=ALU.add)
                last.then_inc(f_ac, 1)
            dve.wait_ge(f_ac, (i + 1) * E)
            dve.wait_ge(f_w, 64)
            gb = gbrow[:, bass.ds(i // 2, 1), :].broadcast_to([P, G, D])
            step(6, v.tensor_tensor(acc[:, 0, :, :], acc[:, 0, :, :], gb, ALU.mult))
            step(7, v.tensor_tensor(acc[:, 1, :, :], acc[:, 0, :, :], x1[:], ALU.add))
            step(8, v.tensor_copy(mx[:], mx[:]))

    @block.tensor
    def _(pe):
        te = nc.tensor
        pe.wait_ge(f_w, 64)
        pe.wait_ge(f_i, 2)
        for e in range(E):
            wait_n = e - 1
            if wait_n > 0:
                pe.wait_ge(f_tc, wait_n)
            for j in range(HC):
                last = te.transpose(ps_t[:, e % 2, j * P:(j + 1) * P], pj_sb[:, e, j * P:(j + 1) * P], ident2[:])
            last.then_inc(f_t, 1)
        pe.wait_ge(f_tc, E)
        pe.wait_ge(f_c, 5)
        for b in range(NB):
            if b >= 2:
                pe.wait_ge(f_tc, E + b - 1)
            te.matmul(ps_t[:, b % 2, 0:D], sb2[:, b, :], wm2[:], start=True, stop=True).then_inc(f_gm, 1)
        with pe.Fori(0, NG) as i:
            pe.wait_ge(f_in, i * 48 + 48)
            pe.wait_ge(f_w, 64)

            def down(e):
                pe.wait_ge(f_sq, i * HM + (e + 1) * HC)
                pe.wait_ge(f_ac, i * E + (e - 1) if e >= 2 else i * E)
                pe.wait_ge(f_w, 64)
                for k in range(G):
                    for j in range(HC):
                        last = te.matmul(ps_y[:, e % 2, k * D:(k + 1) * D], hh[:, e % 2, j, k * P:(k + 1) * P],
                                         pjT[:, e, j, :], start=(j == 0), stop=(j == HC - 1))
                last.then_inc(f_y, 1)
            for e in range(E):
                for j in range(HC):
                    k = e * HC + j
                    pe.wait_ge(f_rl, i * HM + (k - 3) if k >= 4 else i * HM)
                    pe.wait_ge(f_w, 64)
                    te.matmul(ps_h[:, k % 4, :], fc_sb[:, e, j * P:(j + 1) * P], h2T[:],
                              start=True, stop=True).then_inc(f_hm, 1)
                if e:
                    down(e - 1)
            down(E - 1)


_INS = ['L0_attn_x', 'L0_attn_norm_g', 'L0_attn_Wq', 'L0_attn_Wkv', 'L0_attn_Wout', 'L0_attn_out_norm_g',
        'L0_ffn_router_w', 'L0_ffn_expert_fc', 'L0_ffn_expert_proj', 'L0_c', 'L0_wmod']


def kernel(**inputs):
    import numpy as _np
    import concourse.bacc as _bacc
    from concourse import mybir as _mybir
    from concourse.bass_utils import run_bass_kernel_spmd as _run

    nc = _bacc.Bacc("TRN2", target_bir_lowering=False, num_devices=1)
    arrays, args = {}, []
    for name in _INS:
        a = _np.asarray(inputs[name])
        a = _np.ascontiguousarray(a.T if name == 'L0_c' else a)
        arrays[f"in_{name}_dram"] = a
        args.append(nc.dram_tensor(f"in_{name}_dram", a.shape, _mybir.dt.from_np(a.dtype), kind="ExternalInput").ap())
    shape = tuple(inputs['L0_attn_x'].shape)
    args.append(nc.dram_tensor("out_0_dram", shape, F32, kind="ExternalOutput").ap())
    build(nc, *args)
    r = _run(nc, [arrays], core_ids=[0])
    return r.results[0]["out_0_dram"]
```

```python
from contextlib import ExitStack

import concourse.bass as bass
from concourse import mybir

F32 = mybir.dt.float32
F16 = mybir.dt.float16
BF16 = mybir.dt.bfloat16
I32 = mybir.dt.int32
U32 = mybir.dt.uint32
ALU = mybir.AluOpType
ACT = mybir.ActivationFunctionType
AX_X = mybir.AxisListType.X

P = 128
EPS = 1e-5
SCALE = 16.0
LOOK = 2
RING = 4
BR = 8
UP_AHEAD = 2


def build(nc, x, norm_g, wq, wkv, wout, out_g, router, fc, proj, c, wmod, out):
    NB, N, D = x.shape
    H = 8
    INNER = wq.shape[1]
    DH = INNER // H
    E, _, HID = fc.shape
    TB = N // P
    NT = NB * TB
    HT = TB // 2
    HALF = HT * P
    NQK = H + 1
    VC = 2 * DH + 1
    VP = VC + 1
    HC = HID // P
    NS = 8
    assert D == P and DH == 64 and N == 1024 and TB == 8 and 2 * DH == P

    x_t = x.rearrange("b (t p) d -> (b t) p d", p=P)
    NTOK = NB * N
    CAP = NTOK + P
    NBLK = NT + E - 1 + (-(NT + E - 1)) % BR
    W = 3 * D + 4
    TOK = 3 * D
    NOBODY = float(4 * NTOK)
    rows_dram = nc.dram_tensor("routed_rows", (E * CAP + P, W), F32, kind="Internal").ap()
    out_rows = out.rearrange("b n d -> (b n) d")

    with ExitStack() as ctx:
        def sb(name, shape, dt=F32):
            return ctx.enter_context(nc.sbuf_tensor(name, shape, dt))

        def pb(name, shape, dt=F32):
            return ctx.enter_context(nc.psum_tensor(name, shape, dt))

        sems = []

        def sem(name):
            s = ctx.enter_context(nc.semaphore(name))
            sems.append(s)
            return s

        wq_sb = sb("wq_sb", [P, INNER])
        wkv_sb = sb("wkv_sb", [P, 2 * DH])
        wout_sb = sb("wout_sb", [P, INNER // P, D])
        router_sb = sb("router_sb", [E, D])
        routerT = sb("routerT", [P, E])
        g_col = sb("g_col", [P, 1])
        outg_row = sb("outg_row", [P, D])
        c_T = sb("c_T", [P, NB])
        silu_T = sb("silu_T", [P, NB])
        wmod_sb = sb("wmod_sb", [P, 6 * D])
        mod = sb("mod", [P, NB, 6, D])
        ident = sb("ident", [P, P])
        ident16 = sb("ident16", [P, P], F16)
        tick = sb("tick", [P, 1])
        power = sb("power", [P, 16])
        clamp = sb("clamp", [P, NQK])
        rows_a = sb("rows_a", [P, 2, D])
        rows_f = sb("rows_f", [P, 3, D])
        x_in = sb("x_in", [P, D])
        xn_a = sb("xn_a", [P, D])
        hs_a = sb("hs_a", [P, D])
        h_a = sb("h_a", [P, D])
        xhat = sb("xhat", [P, D])
        st_1, st_2 = sb("st_1", [P, 2, 6]), sb("st_2", [P, 2, 6])
        mv_1, mv_2 = sb("mv_1", [P, 2, 2]), sb("mv_2", [P, 2, 2])
        ve_1, ve_2 = sb("ve_1", [P, 2]), sb("ve_2", [P, 2])
        rs_1, rs_2 = sb("rs_1", [P, 2]), sb("rs_2", [P, 2])
        xnT = sb("xnT", [P, P])
        qkv = sb("qkv", [P, INNER + 2 * DH])
        sq = sb("sq", [P, NQK * DH])
        ss = sb("ss", [P, NQK])
        z = sb("z", [P, NQK])
        rq = sb("rq", [P, NQK])
        qn = sb("qn", [P, NQK * DH])
        qs = sb("qs", [P, NQK + 1, 2 * DH], F16)
        q_next = sb("q_next", [P, H, HALF], F16)
        q_cur = sb("q_cur", [P, 2, H, HALF], F16)
        k_next = sb("k_next", [P, 2, N], F16)
        k_cur = sb("k_cur", [P, 2, N], F16)
        v_next = sb("v_next", [P, TB, VP], BF16)
        v_cur = sb("v_cur", [P, TB, VP], BF16)
        probs = sb("probs", [P, RING, 2 * HALF])
        rest = sb("rest", [P, RING, 2 * HALF], BF16)
        o_raw = sb("o_raw", [P, 2, HT, VC])
        silu_b = o_raw[:].rearrange("p a t c -> p (a t c)")[:, 0:NB * P].rearrange("p (b n) -> p b n", b=NB)
        gmag = probs[:].rearrange("p r n -> p (r n)")[:, 0:NB * 2 * D].rearrange("p (b k d) -> p b k d", b=NB, k=2)
        o_rin = sb("o_rin", [P, 2, HT])
        o_sum = sb("o_sum", [P, HT, DH])
        o_all = sb("o_all", [P, 2, HT, INNER])
        oT = sb("oT", [P, INNER // P, P])
        y_o = sb("y_o", [P, D])
        x_res = sb("x_res", [P, D])
        yn = sb("yn", [P, D])
        yg = sb("yg", [P, D])
        pay = sb("pay", [P, 2, W])
        hn = sb("hn", [P, D])
        hc = sb("hc", [P, D])
        h2T = sb("h2T", [P, P])
        lg = sb("lg", [P, E])
        first_pref = sb("first_pref", [P, E])
        e_base = sb("e_base", [P, E])
        below = sb("below", [P, P], BF16)
        ones16 = sb("ones16", [P, P], BF16)
        lg_max = sb("lg_max", [P, 1])
        lg_eq = sb("lg_eq", [P, E])
        eq_max = sb("eq_max", [P, 1])
        chosen = sb("chosen", [P, E])
        chosen16 = sb("chosen16", [P, E], BF16)
        counted = sb("counted", [P, E], BF16)
        place = sb("place", [P, E])
        place_c = sb("place_c", [P, E])
        dest = sb("dest", [P, 1])
        dest_i = sb("dest_i", [P, 1], U32)
        filler = sb("filler", [P, W])
        p_tick = sb("p_tick", [P, 1])
        fc_sb = sb("fc_sb", [P, E, HID])
        fc_lo = sb("fc_lo", [P, E, HID], BF16)
        pjT = sb("pjT", [P, E, HC, D])
        pjT_lo = sb("pjT_lo", [P, E, HC, D], BF16)
        pj_in = o_all[:].rearrange("p a t i -> p (a t i)").rearrange("p (e h) -> p e h", e=E)
        blk_i = sb("blk_i", [P, NBLK], I32)
        blk = sb("blk", [P, NBLK])
        part_i = sb("part_i", [P, 1], I32)
        part = sb("part", [P, 1])
        total = sb("total", [P, E])
        total_i = sb("total_i", [P, E], I32)
        nblk = sb("nblk", [P, E])
        start = sb("start", [P, E + 1])
        jump = sb("jump", [P, E])
        free = o_all[:].rearrange("p a t i -> p (a t i)")
        past = free[:, 0:E * NBLK].rearrange("p (e j) -> p e j", e=E)
        past_j = free[:, E * NBLK:2 * E * NBLK].rearrange("p (e j) -> p e j", e=E)
        relu = free[:, 4 * HID:6 * HID].rearrange("p (k h) -> p k h", k=2)
        act2 = free[:, 6 * HID:8 * HID].rearrange("p (k h) -> p k h", k=2)
        row_f = sb("row_f", [P, NBLK])
        exp_f = sb("exp_f", [P, NBLK])
        row_tab = sb("row_tab", [P, NBLK], I32)
        exp_tab = sb("exp_tab", [P, NBLK], I32)
        fill_i = sb("fill_i", [P, E], U32)
        free = probs[:].rearrange("p r n -> p (r n)")
        b_in = free[:, 0:BR * W].rearrange("p (k w) -> p k w", k=BR)
        act2_lo = rest[:].rearrange("p r n -> p (r n)")[:, 0:2 * HID].rearrange("p (k h) -> p k h", k=2)
        hT = sb("hT", [P, 2, P])
        hT_lo = sb("hT_lo", [P, 2, P], BF16)
        y_g = sb("y_g", [P, 2, D])
        y_fin = sb("y_fin", [P, 4, D])
        tok_i = sb("tok_i", [P, 4, 1], U32)

        ps_s = pb("ps_s", [P, 2, 2, HALF])
        ps_o = pb("ps_o", [P, 2, 512])
        ps_m0 = pb("ps_m0", [P, 512])
        ps_m1 = pb("ps_m1", [P, 512])
        ps_m0h = ps_m0[:].bitcast(F16)
        ps_m1h = ps_m1[:].bitcast(F16)

        s_w = sem("weights_loaded")
        s_id = sem("identity_steps")
        s_const = sem("constants_ready")
        s_silu = sem("silu_steps")
        s_silub = sem("silu_broadcast")
        s_modmm = sem("mod_products")
        s_modcp = sem("mod_copied")
        s_modf = sem("mod_finishing")
        s_modr = sem("mod_ready")
        s_rT = sem("router_transposed")
        s_rowa = sem("rows_a_moved")
        s_rowf = sem("rows_f_moved")
        s_tick = sem("waited")
        s_xin = sem("x_in_loaded")
        s_xres = sem("x_res_loaded")
        s_scores = sem("scores_ready")
        s_exp = sem("exp_done")
        s_rest = sem("rest_ready")
        s_pv = sem("pv_done")
        s_ocp = sem("o_copied")
        s_orin = sem("o_reciprocal")
        s_osum = sem("o_summed")
        s_onorm = sem("o_normed")
        s_kst = sem("k_staged")
        s_vst = sem("v_staged")
        s_qst = sem("q_staged")
        s_kcur = sem("k_moved")
        s_vcur = sem("v_moved")
        s_qcur = sem("q_moved")
        s_ones = sem("ones_set")
        s_ja = sem("xhat_transposed")
        s_xnT = sem("xnT_ready")
        s_jq = sem("q_projected")
        s_jkv = sem("kv_projected")
        s_qcp = sem("q_copied")
        s_kvcp = sem("kv_copied")
        s_jqT = sem("q_transposed")
        s_jkT = sem("k_transposed")
        s_jo = sem("o_transposed")
        s_oT = sem("oT_ready")
        s_jy = sem("y_projected")
        s_y = sem("y_copied")
        s_jh = sem("h2_transposed")
        s_h2T = sem("h2T_ready")
        s_jl = sem("logits_product")
        s_lg = sem("logits_copied")
        s_v1 = sem("variances_1")
        s_r1 = sem("rsqrt_1")
        s_v2 = sem("variances_2")
        s_r2 = sem("rsqrt_2")
        s_xa = sem("xn_a_ready")
        s_ha = sem("h_a_steps")
        s_xh = sem("xhat_ready")
        s_sq = sem("squares_ready")
        s_ss = sem("norms_squared")
        s_rq = sem("rsqrt_q")
        s_qn = sem("qn_ready")
        s_hi = sem("q_hi_ready")
        s_vhi = sem("v_hi_ready")
        s_lo = sem("q_lo_ready")
        s_yn = sem("yn_ready")
        s_x1 = sem("x1_steps")
        s_hn = sem("hn_ready")
        s_h2 = sem("h2_steps")
        s_fw = sem("expert_weights_loaded")
        s_pj = sem("proj_transposed")
        s_pjc = sem("proj_copied")
        s_rc0 = sem("routing_constants")
        s_tok = sem("token_numbers")
        s_rt = sem("choice_steps")
        s_jr = sem("ranks_product")
        s_pl = sem("place_steps")
        s_cnt = sem("counted")
        s_sc = sem("rows_scattered")
        s_ptick = sem("pool_waited")
        f_tot = sem("totals_product")
        f_map = sem("block_map_steps")
        f_fill = sem("blocks_filled")
        f_ld = [sem(f"block_loaded_{k}") for k in range(BR)]
        f_T = sem("block_transposed")
        f_hT = sem("block_hT_copied")
        f_hL = sem("block_hT_lo")
        f_F = sem("up_product")
        f_rl = sem("relu_done")
        f_sq = sem("squared")
        f_gL = sem("act2_lo_ready")
        f_D = sem("down_product")
        f_yg = sem("y_gated")
        f_yf = sem("y_finished")
        f_sc = [sem(f"out_scattered_{k}") for k in range(4)]

        def wait(eng, s, v):
            if not isinstance(v, int) or v > 0:
                eng.wait_ge(s, v)

        def known(v, lo, hi):
            return not isinstance(v, int) or lo <= v < hi

        def cols(ta, rp):
            have = [known(ta, 0, NT), known(rp, 0, NT)]
            return slice(0 if have[0] else 1, 2 if have[1] else 1) if any(have) else None

        def sweep(eng, macro):
            for m in range(TB):
                macro(-1, m)
            for m in range(TB):
                macro(0, m)
            with eng.Fori(1, NB - 1) as b:
                for m in range(TB):
                    macro(b, m)
            for m in range(TB):
                macro(NB - 1, m)
            for m in range(HT + 3):
                macro(NB, m)

        M0_JOBS = [(0, 7, s_qst, 1), (1, 8, s_xnT, 1), (3, 8, s_qcp, 1), (4, -6, s_pl, 3), (6, -4, s_y, 1),
                   (7, -5, s_lg, 1)]
        M1_JOBS = [(0, 7, s_kst, 1), (3, 8, s_kvcp, 1), (4, -4, s_oT, 1), (5, -5, s_h2T, 1)]

        def bank_free(pe, jobs, b, m, slot):
            M = b * TB + m
            if isinstance(b, int):
                for s, o, sm, per in jobs:
                    wait(pe, sm, per * max(0, min(M + o + (s < slot), NT)))
            else:
                s, o, sm, per = ([j for j in jobs if j[0] < slot] or jobs)[-1]
                wait(pe, sm, per * (M + o + (s < slot)))

        def rows_of(b, k0, k1, off=0):
            if isinstance(b, int):
                return mod[:, (b + off) % NB, k0:k1, :]
            return mod[:, bass.ds((b + off) % NB if off else b, 1), k0:k1, :].rearrange("p o k d -> p (o k) d")

        def gate_of(b):
            if isinstance(b, int):
                return mod[:, b, 5, :]
            return mod[:, bass.ds(b, 1), 5, :].rearrange("p o d -> p (o d)")

        def top(ap):
            return ap.bitcast(BF16).rearrange("p (n two) -> p n two", two=2)[:, :, 1]

        def tile_of(ap, b, k):
            if isinstance(b, int):
                return ap[TB * b + k]
            return ap[bass.ds(b * TB + k, 1)].rearrange("o p d -> (o p) d")

        MAP_STEPS = 15 + E
        FILL_STEPS = 3

        def run_blocks(eng, *stages, group=None):
            group = group or (lambda j: None)
            most = max(ahead for _, ahead in stages)

            def turn(j, k):
                for f, ahead in stages:
                    if isinstance(j, int) and not 0 <= j + ahead < NBLK:
                        continue
                    f(j + ahead, (k + ahead) % BR)
            group(0)
            for j in range(-most, BR):
                turn(j, j % BR)
            with eng.Fori(1, NBLK // BR - 1) as i:
                group(BR * i)
                for k in range(BR):
                    turn(BR * i + k, k)
            group(NBLK - BR)
            for k in range(BR):
                turn(NBLK - BR + k, k)

        block = ctx.enter_context(nc.Block())

        @block.sync
        def _(sp):
            loads = [
                (wmod_sb[:], wmod), (c_T[:], c),
                (g_col[:], norm_g.rearrange("(d o) -> d o", o=1)),
                (wq_sb[:], wq), (wkv_sb[:], wkv),
                (wout_sb[:], wout.rearrange("(j p) n -> p j n", p=P)),
                (router_sb[:], router),
                (outg_row[:], out_g.rearrange("(o d) -> o d", o=1).broadcast_to([P, D])),
            ]
            sp.dma_start(x_in[:], x_t[0]).then_inc(s_xin, 16)
            for dst, src in loads:
                sp.dma_start(dst, src).then_inc(s_w, 16)
            sp.dma_start(pj_in, proj.rearrange("e d h -> d e h")).then_inc(s_fw, 16)
            sp.dma_start(fc_sb[:], fc.rearrange("e d h -> d e h")).then_inc(s_fw, 16)

            def macro(b, m):
                M = b * TB + m
                t = M + 9
                if known(t, 1, NT):
                    wait(sp, s_xa, t)
                    if isinstance(b, int):
                        src = x_t[t]
                    elif m == TB - 1:
                        src = x_t[bass.ds(((b + 2) % NB) * TB, 1)].rearrange("o p d -> (o p) d")
                    else:
                        src = tile_of(x_t, b, m + 9)
                    sp.dma_start(x_in[:], src).then_inc(s_xin, 16)
                r = M - 4
                if known(r, 0, NT):
                    wait(sp, s_x1, 2 * r)
                    sp.dma_start(x_res[:], tile_of(x_t, b, m - 4)).then_inc(s_xres, 16)

            sweep(sp, macro)

            def load(j, k):
                wait(sp, f_yf, j + 1 - BR)
                base = sp.value_load(row_tab[0:1, bass.ds(j, 1)] if not isinstance(j, int) else row_tab[0:1, j:j + 1],
                                     min_val=0, max_val=E * CAP)
                sp.dma_start(b_in[:, k, :], rows_dram[bass.ds(base, P), :]).then_inc(f_ld[k], 16)

            sp.wait_ge(f_map, MAP_STEPS)
            sp.wait_ge(s_sc, 16 * NT)
            sp.wait_ge(f_fill, 16 * (E + 1))
            for k in range(BR):
                load(k, k)
            with sp.Fori(1, NBLK // BR) as i:
                for k in range(BR):
                    load(BR * i + k, k)
            for k in range(4):
                sp.wait_ge(f_sc[k], 4 * NBLK)

        @block.gpsimd
        def _(pool):
            g = nc.gpsimd
            g.memset(ident[:], 0.0).then_inc(s_id, 1)
            g.memset(power[:], -0.5)
            g.memset(clamp[:, 0:H], 1e-24 / SCALE ** 2 / 16.0)
            g.memset(clamp[:, H:NQK], 1e-24 / 16.0).then_inc(s_id, 1)
            pool.wait_ge(s_id, 2)
            g.affine_select(out=ident[:], in_=ident[:], compare_op=ALU.not_equal, fill=1.0, base=0,
                            pattern=[[-1, P]], channel_multiplier=1).then_inc(s_id, 1)
            pool.wait_ge(s_id, 3)
            g.tensor_copy(ident16[:], ident[:]).then_inc(s_const, 1)
            for e in range(E):
                g.memset(first_pref[:, e:e + 1], float(E - e))
                g.memset(e_base[:, e:e + 1], float(e * CAP))
            g.memset(below[:], 1.0).then_inc(s_rc0, 1)
            g.memset(ones16[:], 1.0)
            g.memset(counted[:], 0.0)
            g.memset(pay[:], 0.0)
            g.memset(p_tick[:], 0.0)
            g.iota(part_i[:], pattern=[[0, 1]], base=0, channel_multiplier=1)
            g.iota(blk_i[:], pattern=[[1, NBLK]], base=0, channel_multiplier=0)
            g.memset(filler[:], 0.0).then_inc(s_rc0, 1)
            pool.wait_ge(s_rc0, 2)
            g.affine_select(out=below[:], in_=below[:], compare_op=ALU.is_gt, fill=0.0, base=0,
                            pattern=[[1, P]], channel_multiplier=-1)
            g.memset(filler[:, TOK:TOK + 1], NOBODY).then_inc(s_rc0, 1)
            g.memset(v_next[:], 1.0).then_inc(s_ones, 1)
            g.memset(v_cur[:], 1.0).then_inc(s_ones, 1)
            pool.wait_ge(s_ones, 2)
            pool.wait_ge(s_modr, 1)

            def scatter(dst, idx, src, **bounds):
                return g.indirect_dma_start(dst, bass.IndirectOffsetOnAxis(ap=idx, axis=0), src, None, **bounds)

            def macro(b, m):
                M = b * TB + m
                ta, t, r, rp = M + 9, M + 8, M - 4, M - 5
                both = cols(ta, rp)
                if both:
                    wait(pool, s_v1, 3 * (M + 10))
                    g.tensor_tensor(rs_1[:, both], ve_1[:, both], power[:, both], ALU.pow).then_inc(s_r1, 1)

                def norm_o(u, free):
                    wait(pool, s_ocp, u + 1)
                    wait(pool, s_onorm, u)
                    raw = o_raw[:, um, :, :]
                    g.tensor_tensor(o_sum[:], raw[:, :, 0:DH], raw[:, :, DH:2 * DH], ALU.add).then_inc(s_osum, 1)
                    wait(pool, s_osum, u + 1)
                    wait(pool, s_orin, u + 1)
                    if free is not None:
                        wait(pool, s_jo, free)
                    g.tensor_tensor(o_all[:, uh, :, hh * DH:(hh + 1) * DH], o_sum[:],
                                    o_rin[:, um, :].rearrange("p (t o) -> p t o", o=1).broadcast_to([P, HT, DH]),
                                    ALU.mult).then_inc(s_onorm, 1)

                if known(ta, 0, NT):
                    wait(pool, s_xa, ta + 1)
                    if m == TB - 1:
                        wait(pool, s_rowa, b + 3)
                    g.tensor_tensor(hs_a[:], xn_a[:], rows_a[:, 1, :], ALU.mult).then_inc(s_ha, 1)
                    wait(pool, s_ha, 2 * ta + 1)
                    g.tensor_tensor(h_a[:], hs_a[:], rows_a[:, 0, :], ALU.add).then_inc(s_ha, 1)
                if known(rp, 0, NT):
                    wait(pool, s_yn, rp + 1)
                    if m == 5:
                        wait(pool, s_rowf, b + 1)
                    g.tensor_tensor(yg[:], yn[:], rows_f[:, 0, :], ALU.mult).then_inc(s_x1, 1)
                    wait(pool, s_x1, 2 * rp + 1)
                    wait(pool, s_xres, 16 * (rp + 1))
                    wait(pool, s_sc, 16 * (rp - 1))
                    g.tensor_tensor(pay[:, (m - 5) % 2, D:2 * D], yg[:], x_res[:], ALU.add).then_inc(s_x1, 1)
                if known(M - 1, 0, NT):
                    mm = (m - 1) % TB
                    um, uh, hh = 1, mm // 4, 2 * (mm % 4) + 1
                    norm_o(2 * M - 1, None)
                if both:
                    wait(pool, s_v2, 3 * (M + 10))
                    g.tensor_tensor(rs_2[:, both], ve_2[:, both], power[:, both], ALU.pow).then_inc(s_r2, 1)
                if known(t, 0, NT):
                    wait(pool, s_qcp, t + 1)
                    wait(pool, s_kvcp, t + 1)
                    g.tensor_tensor(sq[:], qkv[:, 0:NQK * DH], qkv[:, 0:NQK * DH], ALU.mult).then_inc(s_sq, 1)
                if known(rp, 0, NT):
                    wait(pool, s_hn, rp + 1)
                    g.tensor_tensor(hc[:], hn[:], rows_f[:, 2, :], ALU.mult).then_inc(s_h2, 1)
                    wait(pool, s_h2, 2 * rp + 1)
                    g.tensor_tensor(pay[:, (m - 5) % 2, 0:D], hc[:], rows_f[:, 1, :], ALU.add).then_inc(s_h2, 1)
                if known(M, 0, NT):
                    um, uh, hh = 0, m // 4, 2 * (m % 4)
                    norm_o(2 * M, 4 * (M // 4 - 1) if isinstance(b, int) and m % 4 == 0
                           else (8 * b + 4 * (m // 4 - 1) if m % 4 == 0 else None))
                if known(t, 0, NT):
                    wait(pool, s_ss, 2 * (t + 1))
                    g.tensor_tensor(rq[:], z[:], power[:, 0:NQK], ALU.pow).then_inc(s_rq, 1)
                q = M - 6
                if known(q, 0, NT):
                    wait(pool, s_pl, 3 * (q + 1))
                    wait(pool, s_tok, q + 1)
                    wait(pool, s_ptick, q)
                    g.tensor_tensor(p_tick[:], p_tick[:], p_tick[:], ALU.add).then_inc(s_ptick, 1)
                    scatter(rows_dram, dest_i[:], pay[:, m % 2, :]).then_inc(s_sc, 16)

            pool.wait_ge(s_v1, 3)
            g.tensor_tensor(rs_1[:, 0:1], ve_1[:, 0:1], power[:, 0:1], ALU.pow).then_inc(s_r1, 1)
            pool.wait_ge(s_xa, 1)
            pool.wait_ge(s_rowa, 1)
            g.tensor_tensor(hs_a[:], xn_a[:], rows_a[:, 1, :], ALU.mult).then_inc(s_ha, 1)
            pool.wait_ge(s_ha, 1)
            g.tensor_tensor(h_a[:], hs_a[:], rows_a[:, 0, :], ALU.add).then_inc(s_ha, 1)
            pool.wait_ge(s_v2, 3)
            g.tensor_tensor(rs_2[:, 0:1], ve_2[:, 0:1], power[:, 0:1], ALU.pow).then_inc(s_r2, 1)
            pool.wait_ge(s_rc0, 3)
            pool.dma_start(rows_dram[E * CAP:E * CAP + P, :], filler[:]).then_inc(f_fill, 16)
            sweep(pool, macro)

            pool.wait_ge(f_map, FILL_STEPS)
            for e in range(E):
                scatter(rows_dram, fill_i[:, e:e + 1], filler[:]).then_inc(f_fill, 16)

            def finish(j, k):
                wait(pool, f_yf, j + 1)
                wait(pool, s_ptick, NT + j)
                g.tensor_tensor(p_tick[:], p_tick[:], p_tick[:], ALU.add).then_inc(s_ptick, 1)
                scatter(out_rows, tok_i[:, k % 4, :], y_fin[:, k % 4, :], bounds_check=NTOK - 1, oob_is_err=False
                        ).then_inc(f_sc[k % 4], 16)

            run_blocks(pool, (finish, 0))

        @block.scalar
        def _(act):
            a = nc.scalar
            act.wait_ge(s_w, 16 * 8)
            a.activation(silu_T[:], c_T[:], ACT.Exp, scale=-1.0).then_inc(s_silu, 1)
            for b in range(NB):
                act.wait_ge(s_modmm, b + 1)
                a.copy(mod[:, b, 0:3, :], ps_s[:, b % 2, 0, 0:3 * D].rearrange("p (k d) -> p k d", k=3))
                a.copy(mod[:, b, 3:6, :], ps_s[:, b % 2, 1, 0:3 * D].rearrange("p (k d) -> p k d", k=3)
                       ).then_inc(s_modcp, 1)
            act.wait_ge(s_rT, 1)
            a.copy(routerT[:], ps_m0[:, 0:E]).then_inc(s_modcp, 1)

            def macro(b, m):
                M = b * TB + m
                t, tp, r, rp = M + 8, M + 7, M - 4, M - 5
                if isinstance(b, int) and b < 0:
                    wait(act, s_pj, m + 1)
                    a.copy(pjT[:, m, :, :], ps_s[:, m % 2, 0, :].rearrange("p (j d) -> p j d", j=HC)).then_inc(s_pjc, 1)
                for s in range(NS):
                    X = M * NS + s
                    if s in (1, 5):
                        U = 2 * M - 1 if s == 1 else 2 * M
                        if known(M - (s == 1), 0, NT):
                            wait(act, s_pv, 4 * (U + 1))
                            wait(act, s_onorm, U - 1)
                            par = 1 if s == 1 else 0
                            a.copy(o_raw[:, par, :, :].rearrange("p (k t) d -> p k (t d)", k=2),
                                   ps_o[:, :, 0:2 * VC]).then_inc(s_ocp, 1)
                    if s == 0 and known(tp, 0, NT):
                        qm = (m - 1) % TB
                        wait(act, s_jqT, tp + 1)
                        wait(act, s_qcur, 2 * b + 1 + (1 if m > 4 else 0) if m > 0 else 2 * b)
                        a.copy(q_next[:, :, (qm % HT) * P:(qm % HT + 1) * P],
                               ps_m0h[:, 0:H * P].rearrange("p (h n) -> p h n", h=H)).then_inc(s_qst, 1)
                        wait(act, s_jkT, tp + 1)
                        wait(act, s_kcur, 4 * b + qm // 2 + 1 if m > 0 else 4 * (b - 1) + qm // 2 + 1)
                        a.copy(k_next[:, :, qm * P:(qm + 1) * P],
                               ps_m1h[:, 0:2 * P].rearrange("p (h n) -> p h n", h=2)).then_inc(s_kst, 1)
                    if s == 1 and known(t, 0, NT):
                        wait(act, s_ja, t + 1)
                        wait(act, s_jkv, t)
                        a.activation(xnT[:], ps_m0[:, 0:P], ACT.Copy, scale=g_col[:, 0:1]).then_inc(s_xnT, 1)
                    if s == 3 and known(t, 0, NT):
                        wait(act, s_jq, t + 1)
                        wait(act, s_qn, t)
                        a.copy(qkv[:, 0:INNER], ps_m0[:, 0:INNER]).then_inc(s_qcp, 1)
                        wait(act, s_jkv, t + 1)
                        wait(act, s_vst, t)
                        a.copy(qkv[:, INNER:INNER + 2 * DH], ps_m1[:, 0:2 * DH]).then_inc(s_kvcp, 1)
                    if s == 4 and known(r, 0, NT):
                        wait(act, s_jo, r + 1)
                        wait(act, s_jy, r)
                        a.copy(oT[:], ps_m1[:].rearrange("p (j n) -> p j n", n=P)).then_inc(s_oT, 1)
                    if s == 6 and known(r, 0, NT):
                        wait(act, s_jy, r + 1)
                        wait(act, s_yn, r)
                        a.copy(y_o[:], ps_m0[:, 0:D]).then_inc(s_y, 1)
                    if s == 5 and known(rp, 0, NT):
                        wait(act, s_jh, rp + 1)
                        wait(act, s_jl, rp)
                        a.copy(h2T[:], ps_m1[:, 0:P]).then_inc(s_h2T, 1)
                    if s == 7 and known(rp, 0, NT):
                        wait(act, s_jl, rp + 1)
                        wait(act, s_rt, 4 * rp)
                        a.copy(lg[:], ps_m0[:, 0:E]).then_inc(s_lg, 1)
                    if s == 7 and known(t, 0, NT):
                        wait(act, s_qn, t + 1)
                        wait(act, s_jqT, t)
                        wait(act, s_jkT, t)
                        qn3 = qn[:].rearrange("p (h d) -> p h d", d=DH)
                        a.copy(qs[:, 0:NQK, 0:DH], qn3)
                        a.copy(qs[:, H, DH:2 * DH], qn3[:, H, :]).then_inc(s_hi, 1)
                        wait(act, s_vcur, 4 * b + m // 2 + 1)
                        wait(act, s_ones, 1)
                        a.copy(v_next[:, m, 0:DH], qkv[:, NQK * DH:(NQK + 1) * DH]).then_inc(s_vhi, 1)
                    if known(X + LOOK, 0, NT * NS):
                        k = (s + LOOK) % NS
                        wait(act, s_scores, X + LOOK + 1)
                        wait(act, s_pv, X + LOOK - RING + 1)
                        a.activation(probs[:, k % RING, :], ps_s[:, k % 2, :, :].rearrange("p k n -> p (k n)"),
                                     ACT.Exp).then_inc(s_exp, 1)

            sweep(act, macro)

            def copy_hT(j, k):
                wait(act, f_T, j + 1)
                wait(act, f_F, j - 1)
                wait(act, f_hL, j - 1)
                a.copy(hT[:, k % 2, :], ps_o[:, k % 2, 0:P]).then_inc(f_hT, 1)

            def do_relu(j, k):
                wait(act, f_F, j + 1)
                wait(act, f_sq, j - 1)
                a.activation(relu[:, k % 2, :], ps_s[:, 0, k % 2, :], ACT.Relu).then_inc(f_rl, 1)

            def square(j, k):
                wait(act, f_rl, j + 1)
                wait(act, f_D, j - 1)
                wait(act, f_gL, j - 1)
                a.activation(act2[:, k % 2, :], relu[:, k % 2, :], ACT.Square).then_inc(f_sq, 1)

            run_blocks(act, (copy_hT, 3), (do_relu, UP_AHEAD), (square, UP_AHEAD))

        @block.vector
        def _(dve):
            v = nc.vector
            dve.wait_ge(s_silu, 1)
            v.tensor_scalar_add(silu_T[:], silu_T[:], 1.0).then_inc(s_silu, 1)
            dve.wait_ge(s_silu, 2)
            v.reciprocal(silu_T[:], silu_T[:]).then_inc(s_silu, 1)
            dve.wait_ge(s_silu, 3)
            v.tensor_tensor(silu_T[:], silu_T[:], c_T[:], ALU.mult).then_inc(s_silu, 1)
            dve.wait_ge(s_silu, 4)
            v.tensor_copy(silu_b, silu_T[:].rearrange("p (b o) -> p b o", o=1).broadcast_to([P, NB, P])
                          ).then_inc(s_silub, 1)
            dve.wait_ge(s_modcp, NB)
            n = [0]

            def link(ins):
                n[0] += 1
                ins.then_inc(s_modf, 1)
                dve.wait_ge(s_modf, n[0])
            link(v.tensor_scalar_add(mod[:, :, 1, :], mod[:, :, 1, :], 1.0))
            link(v.tensor_scalar_add(mod[:, :, 4, :], mod[:, :, 4, :], 1.0))
            for j, k in ((0, 2), (1, 5)):
                link(v.tensor_scalar(gmag[:, :, 0, :], mod[:, :, k, :], -1.0, 0.25, ALU.mult, ALU.max))
                link(v.tensor_tensor(gmag[:, :, 0, :], gmag[:, :, 0, :], mod[:, :, k, :], ALU.max))
                link(v.tensor_scalar(gmag[:, :, 1, :], mod[:, :, k, :], 0.0, 2.0, ALU.is_ge, ALU.mult))
                link(v.tensor_scalar_add(gmag[:, :, 1, :], gmag[:, :, 1, :], -1.0))
                link(v.tensor_tensor(mod[:, :, k, :], gmag[:, :, 0, :], gmag[:, :, 1, :], ALU.mult))
            v.tensor_tensor(mod[:, :, 2, :], mod[:, :, 2, :],
                            outg_row[:].rearrange("p (o d) -> p o d", o=1).broadcast_to([P, NB, D]),
                            ALU.mult).then_inc(s_modr, 1)

            def stats(srcs, both, st, mv, ve, chain, i):
                for k, src in srcs:
                    last = v.bn_stats(st[:, k, :], src)
                last.then_inc(chain, 1)
                wait(dve, chain, 3 * i + 1)
                v.tensor_scalar_add(tick[:], power[:, 0:1], 1.0)
                for k, src in srcs:
                    last = v.bn_aggr(mv[:, k, :], st[:, k, :])
                last.then_inc(chain, 1)
                wait(dve, chain, 3 * i + 2)
                v.tensor_scalar_add(ve[:, both], mv[:, both, 1], EPS).then_inc(chain, 1)

            def normed(dst, src, mv, rs, k, done):
                v.tensor_scalar(dst[:], src, mv[:, k, 0:1], rs[:, k:k + 1], ALU.subtract, ALU.mult).then_inc(done, 1)

            def x1_of(m):
                return pay[:, (m - 5) % 2, D:2 * D]

            def stats_1(i, a, c):
                srcs = []
                if known(a, 0, NT):
                    wait(dve, s_xin, 16 * (a + 1))
                    srcs.append((0, x_in[:]))
                if known(c, 0, NT):
                    wait(dve, s_y, c + 1)
                    srcs.append((1, y_o[:]))
                stats(srcs, cols(a, c), st_1, mv_1, ve_1, s_v1, i)

            def stats_2(i, a, c, m):
                srcs = []
                if known(a, 0, NT):
                    wait(dve, s_ha, 2 * (a + 1))
                    srcs.append((0, h_a[:]))
                if known(c, 0, NT):
                    wait(dve, s_x1, 2 * (c + 1))
                    srcs.append((1, x1_of(m)))
                stats(srcs, cols(a, c), st_2, mv_2, ve_2, s_v2, i)

            def norm_1(i, a, c):
                wait(dve, s_r1, i + 1)
                wait(dve, s_v1, 3 * (i + 1))
                if known(a, 0, NT):
                    wait(dve, s_ha, 2 * a)
                    normed(xn_a, x_in[:], mv_1, rs_1, 0, s_xa)
                if known(c, 0, NT):
                    wait(dve, s_x1, 2 * c)
                    normed(yn, y_o[:], mv_1, rs_1, 1, s_yn)

            def norm_2(i, a, c, m):
                wait(dve, s_r2, i + 1)
                wait(dve, s_v2, 3 * (i + 1))
                if known(a, 0, NT):
                    wait(dve, s_ja, a)
                    normed(xhat, h_a[:], mv_2, rs_2, 0, s_xh)
                if known(c, 0, NT):
                    wait(dve, s_h2, 2 * c)
                    normed(hn, x1_of(m), mv_2, rs_2, 1, s_hn)

            dve.wait_ge(s_rc0, 3)
            v.tensor_copy(blk[:], blk_i[:])
            v.tensor_copy(part[:], part_i[:]).then_inc(s_rc0, 1)
            dve.wait_ge(s_rc0, 4)
            v.tensor_scalar_add(pay[:, 0, TOK:TOK + 1], part[:], 0.0)
            v.tensor_scalar_add(pay[:, 1, TOK:TOK + 1], part[:], float(P)).then_inc(s_rc0, 1)
            dve.wait_ge(s_rc0, 5)
            dve.wait_ge(s_const, 1)
            dve.wait_ge(s_modr, 1)
            v.tensor_scalar(rows_a[:], rows_of(0, 0, 2), 1.0, None, ALU.mult).then_inc(s_rowa, 1)
            stats_1(0, 0, -1)
            norm_1(0, 0, -1)
            stats_2(0, 0, -1, 0)
            norm_2(0, 0, -1, 0)

            def macro(b, m):
                M = b * TB + m
                ta, t, r, rp = M + 9, M + 8, M - 4, M - 5
                if isinstance(b, int) and b < 0:
                    dve.wait_ge(s_fw, 32)
                    v.tensor_tensor(fc_lo[:, m, :], fc_sb[:, m, :], top(fc_sb[:, m, :]), ALU.subtract)
                    wait(dve, s_pjc, m + 1)
                    pj = pjT[:, m, :, :].rearrange("p j d -> p (j d)")
                    v.tensor_tensor(pjT_lo[:, m, :, :].rearrange("p j d -> p (j d)"), pj, top(pj), ALU.subtract)
                for s in range(NS):
                    X = M * NS + s
                    if m == 0 and s < 4 and known(b, 0, NB):
                        wait(dve, s_vst, TB * b + 2 * s + 2)
                        wait(dve, s_pv, (b - 1) * TB * NS + TB * NS - 3 + s)
                        wait(dve, s_ones, 2)
                        v.tensor_copy(v_cur[:, 2 * s:2 * s + 2, :], v_next[:, 2 * s:2 * s + 2, :]).then_inc(s_vcur, 1)
                    if known(X, 0, NT * NS):
                        wait(dve, s_exp, X + 1)
                        wait(dve, s_pv, X - RING + 1)
                        pr = probs[:, s % RING, :]
                        hi = pr.bitcast(BF16).rearrange("p (n two) -> p n two", two=2)[:, :, 1]
                        v.tensor_tensor(rest[:, s % RING, :], pr, hi, ALU.subtract).then_inc(s_rest, 1)

                    def k_move(bn, j):
                        wait(dve, s_kst, TB * bn + 2 * j + 2)
                        wait(dve, s_scores, (bn - 1) * TB * NS + TB * NS - 3 + j)
                        v.tensor_copy(k_cur[:, :, 2 * j * P:(2 * j + 2) * P],
                                      k_next[:, :, 2 * j * P:(2 * j + 2) * P]).then_inc(s_kcur, 1)

                    def q_move(bn, half):
                        wait(dve, s_qst, TB * bn + HT * (half + 1))
                        wait(dve, s_scores, (bn - 1) * TB * NS + 4 * NS * (half + 1))
                        v.tensor_copy(q_cur[:, half, :, :], q_next[:]).then_inc(s_qcur, 1)

                    if m == TB - 1 and s in (5, 6, 7) and known(b + 1, 0, NB):
                        k_move(b + 1, s - 5)
                    if m == 0 and s == 1 and known(b, 0, NB):
                        k_move(b, 3)
                        q_move(b, 1)
                    if m == 4 and s == 2 and known(b + 1, 0, NB):
                        q_move(b + 1, 0)

                    if s == 0:
                        if m == TB - 1 and known(ta, 0, NT):
                            wait(dve, s_ha, 2 * ta)
                            v.tensor_scalar(rows_a[:], rows_of(b, 0, 2, 2), 1.0, None, ALU.mult).then_inc(s_rowa, 1)
                        if m == 5 and known(rp, 0, NT):
                            wait(dve, s_h2, 2 * rp)
                            v.tensor_scalar(rows_f[:], rows_of(b, 2, 5), 1.0, None, ALU.mult).then_inc(s_rowf, 1)
                        if m in (5, 6) and known(rp, 0, NT):
                            wait(dve, s_sc, 16 * (rp - 1))
                            v.tensor_scalar(pay[:, m - 5, 2 * D:3 * D], gate_of(b), 1.0, None, ALU.mult)
                        if known(rp, 0, NT):
                            wait(dve, s_sc, 16 * (rp - 1))
                            tok = pay[:, (m - 5) % 2, TOK:TOK + 1]
                            if known(rp, 2, NT):
                                v.tensor_scalar_add(tok, tok, 2.0 * P).then_inc(s_tok, 1)
                            else:
                                v.tensor_scalar_add(tick[:], power[:, 0:1], 1.0).then_inc(s_tok, 1)
                        if cols(ta, rp):
                            stats_1(M + 9, ta, rp)
                    if s == 1 and cols(ta, rp):
                        norm_1(M + 9, ta, rp)
                    if s in (1, 5):
                        U = 2 * M - 1 if s == 1 else 2 * M
                        if known(M - (s == 1), 0, NT):
                            par = 1 if s == 1 else 0
                            wait(dve, s_ocp, U + 1)
                            wait(dve, s_onorm, U - 1)
                            v.reciprocal(o_rin[:, par, :], o_raw[:, par, :, 2 * DH]).then_inc(s_orin, 1)
                    if s == 3 and cols(ta, rp):
                        stats_2(M + 9, ta, rp, m)
                    if s == 4 and cols(ta, rp):
                        norm_2(M + 9, ta, rp, m)
                    q = M - 6
                    if s == 2 and known(q, 0, NT):
                        wait(dve, s_lg, q + 1)
                        wait(dve, s_pl, 3 * q)
                        v.tensor_reduce(lg_max[:], lg[:], AX_X, ALU.max).then_inc(s_rt, 1)
                        wait(dve, s_rt, 4 * q + 1)
                        v.scalar_tensor_tensor(out=lg_eq[:], in0=lg[:], scalar=lg_max[:, 0:1], in1=first_pref[:],
                                               op0=ALU.is_ge, op1=ALU.mult).then_inc(s_rt, 1)
                        wait(dve, s_rt, 4 * q + 2)
                        v.tensor_reduce(eq_max[:], lg_eq[:], AX_X, ALU.max).then_inc(s_rt, 1)
                        wait(dve, s_rt, 4 * q + 3)
                        wait(dve, s_cnt, q)
                        v.tensor_scalar(chosen[:], lg_eq[:], eq_max[:, 0:1], None, ALU.is_equal)
                        v.tensor_scalar(chosen16[:], lg_eq[:], eq_max[:, 0:1], None, ALU.is_equal).then_inc(s_rt, 1)
                    if s == 5 and known(q, 0, NT):
                        wait(dve, s_jr, q + 1)
                        v.tensor_tensor(place[:], ps_m0[:, 0:E], e_base[:], ALU.add).then_inc(s_pl, 1)
                        v.tensor_tensor(counted[:], counted[:], chosen16[:], ALU.add).then_inc(s_cnt, 1)
                        wait(dve, s_pl, 3 * q + 1)
                        v.tensor_tensor_reduce(place_c[:], place[:], chosen[:], 1.0, 0.0, ALU.mult, ALU.add,
                                               dest[:]).then_inc(s_pl, 1)
                        wait(dve, s_pl, 3 * q + 2)
                        wait(dve, s_sc, 16 * q)
                        v.tensor_copy(dest_i[:], dest[:]).then_inc(s_pl, 1)
                    if known(t, 0, NT):
                        qn3 = qn[:].rearrange("p (h d) -> p h d", d=DH)
                        if s == 5:
                            wait(dve, s_sq, t + 1)
                            v.tensor_reduce(ss[:], sq[:].rearrange("p (h d) -> p h d", d=DH), AX_X,
                                            ALU.add).then_inc(s_ss, 1)
                            wait(dve, s_ss, 2 * t + 1)
                            v.scalar_tensor_tensor(out=z[:], in0=ss[:], scalar=1.0 / SCALE, in1=clamp[:],
                                                   op0=ALU.mult, op1=ALU.max).then_inc(s_ss, 1)
                        if s == 6:
                            wait(dve, s_rq, t + 1)
                            wait(dve, s_kvcp, t + 1)
                            v.tensor_tensor(qn3, qkv[:, 0:NQK * DH].rearrange("p (h d) -> p h d", d=DH),
                                            rq[:].rearrange("p (h o) -> p h o", o=1).broadcast_to([P, NQK, DH]),
                                            ALU.mult).then_inc(s_qn, 1)
                        if s == 7:
                            wait(dve, s_hi, t + 1)
                            v.tensor_tensor(qs[:, 0:H, DH:2 * DH], qn3[:, 0:H, :], qs[:, 0:H, 0:DH], ALU.subtract)
                            v.tensor_tensor(qs[:, H + 1, 0:DH], qn3[:, H, :], qs[:, H, 0:DH], ALU.subtract)
                            v.tensor_tensor(qs[:, H + 1, DH:2 * DH], qn3[:, H, :], qs[:, H, 0:DH],
                                            ALU.subtract).then_inc(s_lo, 1)
                            wait(dve, s_vhi, t + 1)
                            v.tensor_tensor(v_next[:, m, DH:2 * DH], qkv[:, NQK * DH:(NQK + 1) * DH],
                                            v_next[:, m, 0:DH], ALU.subtract).then_inc(s_vst, 1)

            sweep(dve, macro)

            n = [0]

            def step(ins):
                n[0] += 1
                ins.then_inc(f_map, 1)
                dve.wait_ge(f_map, n[0])
            dve.wait_ge(f_tot, 1)
            step(v.tensor_copy(total[:], ps_m1[:, 0:E]))
            step(v.scalar_tensor_tensor(out=place[:], in0=total[:], scalar=part[:, 0:1], in1=e_base[:],
                                        op0=ALU.add, op1=ALU.add))
            step(v.tensor_copy(fill_i[:], place[:]))
            assert n[0] == FILL_STEPS
            step(v.tensor_scalar_add(total_i[:], total[:], float(P - 1)))
            step(v.tensor_scalar(total_i[:], total_i[:], 7, None, ALU.logical_shift_right))
            step(v.tensor_copy(nblk[:], total_i[:]))
            step(v.memset(start[:, 0:1], 0.0))
            for e in range(E):
                step(v.tensor_tensor(start[:, e + 1:e + 2], start[:, e:e + 1], nblk[:, e:e + 1], ALU.add))
            step(v.tensor_scalar(jump[:], nblk[:], -float(P), float(CAP), ALU.mult, ALU.add))
            over_e = blk[:].rearrange("p (o j) -> p o j", o=1).broadcast_to([P, E, NBLK])

            def over_j(ap):
                return ap.rearrange("p (e o) -> p e o", o=1).broadcast_to([P, E, NBLK])
            step(v.tensor_tensor(past, over_e, over_j(start[:, 1:E + 1]), ALU.is_ge))
            step(v.tensor_tensor(past_j, past, over_j(jump[:]), ALU.mult))
            step(v.tensor_reduce(exp_f[:], past.rearrange("p e j -> p j e"), AX_X, ALU.add))
            step(v.tensor_reduce(row_f[:], past_j.rearrange("p e j -> p j e"), AX_X, ALU.add))
            step(v.scalar_tensor_tensor(out=row_f[:], in0=blk[:], scalar=float(P), in1=row_f[:],
                                        op0=ALU.mult, op1=ALU.add))
            step(v.tensor_scalar(exp_tab[:], exp_f[:], float(E - 1), float(HID), ALU.min, ALU.mult))
            step(v.tensor_scalar(row_tab[:], row_f[:], float(E * CAP), None, ALU.min))
            assert n[0] == MAP_STEPS, n[0]

            def split_hT(j, k):
                wait(dve, f_hT, j + 1)
                wait(dve, f_F, j - 1)
                v.tensor_tensor(hT_lo[:, k % 2, :], hT[:, k % 2, :], top(hT[:, k % 2, :]), ALU.subtract
                                ).then_inc(f_hL, 1)

            def split_act(j, k):
                wait(dve, f_sq, j + 1)
                wait(dve, f_D, j - 1)
                v.tensor_tensor(act2_lo[:, k % 2, :], act2[:, k % 2, :], top(act2[:, k % 2, :]), ALU.subtract
                                ).then_inc(f_gL, 1)

            def finish(j, k):
                wait(dve, f_sc[k % 4], 4 * (j - k % 4))
                wait(dve, f_ld[k], 16 // BR * (j - k) + 16)
                v.tensor_copy(tok_i[:, k % 4, :], b_in[:, k, TOK:TOK + 1])
                wait(dve, f_D, j + 1)
                bank = (ps_m0, ps_m1)[k % 2]
                v.tensor_tensor(y_g[:, k % 2, :], bank[:, 0:D], b_in[:, k, 2 * D:3 * D], ALU.mult).then_inc(f_yg, 1)
                wait(dve, f_yg, j + 1)
                v.tensor_tensor(y_fin[:, k % 4, :], y_g[:, k % 2, :], b_in[:, k, D:2 * D], ALU.add).then_inc(f_yf, 1)

            run_blocks(dve, (split_hT, 3), (finish, 0), (split_act, UP_AHEAD))

        @block.tensor
        def _(pe):
            te = nc.tensor
            pe.wait_ge(s_silub, 1)
            for b in range(NB):
                wait(pe, s_modcp, b - 1)
                te.matmul(ps_s[:, b % 2, 0, 0:3 * D], silu_b[:, b, :], wmod_sb[:, 0:3 * D], start=True, stop=True)
                te.matmul(ps_s[:, b % 2, 1, 0:3 * D], silu_b[:, b, :], wmod_sb[:, 3 * D:6 * D],
                          start=True, stop=True).then_inc(s_modmm, 1)
            pe.wait_ge(s_const, 1)
            te.transpose(ps_m0[:, 0:E], router_sb[:], ident[0:E, 0:E]).then_inc(s_rT, 1)
            pe.wait_ge(s_modcp, NB + 1)

            def macro(b, m):
                M = b * TB + m
                t, tp, r, rp = M + 8, M + 7, M - 4, M - 5
                if isinstance(b, int) and b < 0:
                    pe.wait_ge(s_fw, 32)
                    wait(pe, s_pjc, m - 1)
                    for j in range(HC):
                        last = te.transpose(ps_s[:, m % 2, 0, j * P:(j + 1) * P], pj_in[:, m, j * P:(j + 1) * P], ident[:])
                    last.then_inc(s_pj, 1)
                for s in range(NS):
                    X = M * NS + s
                    if s == 0 and known(tp, 0, NT):
                        wait(pe, s_lo, tp + 1)
                        bank_free(pe, M0_JOBS, b, m, s)
                        for h in range(H):
                            last = te.transpose(ps_m0h[:, h * P:(h + 1) * P], qs[:, h, :], ident16[:])
                        last.then_inc(s_jqT, 1)
                        bank_free(pe, M1_JOBS, b, m, s)
                        for j in range(2):
                            last = te.transpose(ps_m1h[:, j * P:(j + 1) * P], qs[:, H + j, :], ident16[:])
                        last.then_inc(s_jkT, 1)
                    if s == 1 and known(t, 0, NT):
                        wait(pe, s_xh, t + 1)
                        bank_free(pe, M0_JOBS, b, m, s)
                        te.transpose(ps_m0[:, 0:P], xhat[:], ident[:]).then_inc(s_ja, 1)
                    if s == 3 and known(t, 0, NT):
                        wait(pe, s_xnT, t + 1)
                        bank_free(pe, M0_JOBS, b, m, s)
                        te.matmul(ps_m0[:, 0:INNER], xnT[:], wq_sb[:], start=True, stop=True).then_inc(s_jq, 1)
                        bank_free(pe, M1_JOBS, b, m, s)
                        te.matmul(ps_m1[:, 0:2 * DH], xnT[:], wkv_sb[:], start=True, stop=True).then_inc(s_jkv, 1)
                    if s == 4 and known(r, 0, NT):
                        wait(pe, s_onorm, 8 * (r // 4 + 1) if isinstance(b, int)
                             else 16 * b + 8 * ((m - 4) // 4 + 1))
                        bank_free(pe, M1_JOBS, b, m, s)
                        g_par = ((m - 4) // 4) % 2
                        for j in range(INNER // P):
                            last = te.transpose(ps_m1[:, j * P:(j + 1) * P], o_all[:, g_par, (m - 4) % 4, j * P:(j + 1) * P],
                                                ident[:])
                        last.then_inc(s_jo, 1)
                    if s == 4 and known(M - 6, 0, NT):
                        wait(pe, s_rt, 4 * (M - 5))
                        wait(pe, s_cnt, M - 6)
                        bank_free(pe, M0_JOBS, b, m, s)
                        te.matmul(ps_m0[:, 0:E], below[:], chosen16[:], start=True, stop=False)
                        te.matmul(ps_m0[:, 0:E], ones16[:], counted[:], start=False, stop=True).then_inc(s_jr, 1)
                    if s == 5 and known(rp, 0, NT):
                        wait(pe, s_h2, 2 * (rp + 1))
                        bank_free(pe, M1_JOBS, b, m, s)
                        te.transpose(ps_m1[:, 0:P], pay[:, (m - 5) % 2, 0:D], ident[:]).then_inc(s_jh, 1)
                    if s == 6 and known(r, 0, NT):
                        wait(pe, s_oT, r + 1)
                        bank_free(pe, M0_JOBS, b, m, s)
                        for j in range(INNER // P):
                            last = te.matmul(ps_m0[:, 0:D], oT[:, j, :], wout_sb[:, j, :], start=(j == 0),
                                             stop=(j == INNER // P - 1))
                        last.then_inc(s_jy, 1)
                    if s == 7 and known(rp, 0, NT):
                        wait(pe, s_h2T, rp + 1)
                        bank_free(pe, M0_JOBS, b, m, s)
                        te.matmul(ps_m0[:, 0:E], h2T[:], routerT[:], start=True, stop=True).then_inc(s_jl, 1)

                    if known(X + LOOK, 0, NT * NS):
                        s2 = s + LOOK
                        m2 = m + s2 // NS
                        s2 %= NS
                        bo, m2 = m2 // TB, m2 % TB
                        half, h, jj = m2 // 4, 2 * (m2 % 4) + s2 // 4, s2 % 4
                        if known(X, -LOOK, 0) and isinstance(X, int):
                            wait(pe, s_pjc, E)
                        if m2 % 4 == 0 and s2 == 0:
                            wait(pe, s_qcur, 2 * (b + bo) + half + 1)
                        if m2 == 0 and s2 < 4:
                            wait(pe, s_kcur, 4 * (b + bo) + jj + 1)
                        wait(pe, s_exp, X + LOOK - 1)
                        for jc in range(2):
                            for part in range(2):
                                ch = 2 * jj + jc
                                last = te.matmul(ps_s[:, s2 % 2, jc, :], k_cur[:, part, ch * P:(ch + 1) * P],
                                                 q_cur[:, half, h, :], start=(part == 0), stop=(part == 1))
                        last.then_inc(s_scores, 1)
                    if known(X - 1, 0, NT * NS):
                        s1 = (s - 1) % NS
                        m1 = (m - (s == 0)) % TB
                        jj = s1 % 4
                        if m1 == 0 and s1 < 4:
                            wait(pe, s_vcur, 4 * b + jj + 1)
                        if jj == 0:
                            wait(pe, s_ocp, 2 * M + s1 // 4)
                        wait(pe, s_rest, X)
                        for jc in range(2):
                            for it in range(HT):
                                o = ps_o[:, it // 2, (it % 2) * VC:(it % 2 + 1) * VC]
                                vv = v_cur[:, 2 * jj + jc, 0:VC]
                                cols_ = slice(jc * HALF + it * P, jc * HALF + (it + 1) * P)
                                te.matmul(o, top(probs[:, s1 % RING, :])[:, cols_], vv,
                                          start=(jj == 0 and jc == 0 and it % 2 == 0),
                                          stop=False, skip_group_check=True)
                                last = te.matmul(o, rest[:, s1 % RING, cols_], vv, start=False,
                                                 stop=(jj == 3 and jc == 1), skip_group_check=True)
                        last.then_inc(s_pv, 1)

            sweep(pe, macro)

            pe.wait_ge(s_cnt, NT)
            bank_free(pe, M1_JOBS, NB + 1, 0, 0)
            te.matmul(ps_m1[:, 0:E], ones16[:], counted[:], start=True, stop=True).then_inc(f_tot, 1)
            pe.wait_ge(f_map, MAP_STEPS)

            experts = []

            def load_experts(j):
                n = BR if isinstance(j, int) and j > 0 else BR + UP_AHEAD
                tab = exp_tab[0:1, j:j + n] if isinstance(j, int) else exp_tab[0:1, bass.ds(j, n)]
                experts[:] = nc.values_load_multi_w_load_instructions(
                    tab, engines=[mybir.EngineType.PE], min_val=0, max_val=(E - 1) * HID)[1]

            fc_flat = fc_sb[:].rearrange("p e h -> p (e h)")
            fc_top, fc_low = top(fc_flat), fc_lo[:].rearrange("p e h -> p (e h)")
            pj_top = top(pjT[:].rearrange("p e j d -> p (e j d)"))
            pj_low = pjT_lo[:].rearrange("p e j d -> p (e j d)")

            def turn_rows(j, k):
                wait(pe, f_ld[k], 16 // BR * (j - k) + 16)
                wait(pe, f_hT, j - 1)
                te.transpose(ps_o[:, k % 2, 0:P], b_in[:, k, 0:D], ident[:]).then_inc(f_T, 1)

            def up(j, k):
                e = experts[k + BR if k < UP_AHEAD and j is not k else k]
                wait(pe, f_hL, j + 1)
                wait(pe, f_rl, j - 1)
                for c4 in range(HC):
                    for n, w in enumerate((fc_top, fc_low)):
                        wc = w[:, bass.ds(e + c4 * P, P)]
                        te.matmul(ps_s[:, 0, k % 2, c4 * P:(c4 + 1) * P], wc, top(hT[:, k % 2, :]),
                                  start=(n == 0), stop=False)
                        last = te.matmul(ps_s[:, 0, k % 2, c4 * P:(c4 + 1) * P], wc, hT_lo[:, k % 2, :],
                                         start=False, stop=(n == 1))
                last.then_inc(f_F, 1)

            def down(j, k):
                e = experts[k]
                wait(pe, f_gL, j + 1)
                wait(pe, f_yg, j - 1)
                bank = (ps_m0, ps_m1)[k % 2]
                for c4 in range(HC):
                    cols = slice(c4 * P, (c4 + 1) * P)
                    for n, g2 in enumerate((top(act2[:, k % 2, :])[:, cols], act2_lo[:, k % 2, cols])):
                        for i, w in enumerate((pj_top, pj_low)):
                            last = te.matmul(bank[:, 0:D], g2, w[:, bass.ds(e + c4 * P, P)],
                                             start=(c4 == 0 and n == 0 and i == 0),
                                             stop=(c4 == HC - 1 and n == 1 and i == 1))
                last.then_inc(f_D, 1)

            run_blocks(pe, (turn_rows, 3), (up, UP_AHEAD), (down, 0), group=load_experts)


_INS = ['L0_attn_x', 'L0_attn_norm_g', 'L0_attn_Wq', 'L0_attn_Wkv', 'L0_attn_Wout', 'L0_attn_out_norm_g',
        'L0_ffn_router_w', 'L0_ffn_expert_fc', 'L0_ffn_expert_proj', 'L0_c', 'L0_wmod']


def kernel(**inputs):
    import numpy as _np
    import concourse.bacc as _bacc
    from concourse import mybir as _mybir
    from concourse.bass_utils import run_bass_kernel_spmd as _run

    nc = _bacc.Bacc("TRN2", target_bir_lowering=False, num_devices=1)
    arrays, args = {}, []
    for name in _INS:
        a = _np.asarray(inputs[name])
        a = _np.ascontiguousarray(a.T if name == 'L0_c' else a)
        arrays[f"in_{name}_dram"] = a
        args.append(nc.dram_tensor(f"in_{name}_dram", a.shape, _mybir.dt.from_np(a.dtype), kind="ExternalInput").ap())
    shape = tuple(inputs['L0_attn_x'].shape)
    args.append(nc.dram_tensor("out_0_dram", shape, F32, kind="ExternalOutput").ap())
    build(nc, *args)
    r = _run(nc, [arrays], core_ids=[0])
    return r.results[0]["out_0_dram"]
```

```python
from contextlib import ExitStack

import concourse.bass as bass
from concourse import mybir

F32 = mybir.dt.float32
F16 = mybir.dt.float16
BF16 = mybir.dt.bfloat16
I32 = mybir.dt.int32
U32 = mybir.dt.uint32
ALU = mybir.AluOpType
ACT = mybir.ActivationFunctionType
AX_X = mybir.AxisListType.X

P = 128
EPS = 1e-5
SCALE = 16.0
LOOK = 2
RING = 4
BR = 8
WORD = 4
UP_AHEAD = 2


def build(nc, x, norm_g, wq, wkv, wout, out_g, router, fc, proj, c, wmod, out):
    NB, N, D = x.shape
    H = 8
    INNER = wq.shape[1]
    DH = INNER // H
    E, _, HID = fc.shape
    TB = N // P
    NT = NB * TB
    HT = TB // 2
    HALF = HT * P
    NQK = H + 1
    VC = 2 * DH + 1
    VP = VC + 1
    HC = HID // P
    NS = 8
    assert D == P and DH == 64 and N == 1024 and TB == 8 and 2 * DH == P

    x_t = x.rearrange("b (t p) d -> (b t) p d", p=P)
    NTOK = NB * N
    CAP = NTOK + P
    NBLK = NT + E - 1 + (-(NT + E - 1)) % BR
    W = 3 * D + 4
    TOK = 3 * D
    NOBODY = float(4 * NTOK)
    rows_dram = nc.dram_tensor("routed_rows", (E * CAP + P, W), F32, kind="Internal").ap()
    out_rows = out.rearrange("b n d -> (b n) d")

    with ExitStack() as ctx:
        def sb(name, shape, dt=F32):
            return ctx.enter_context(nc.sbuf_tensor(name, shape, dt))

        def pb(name, shape, dt=F32):
            return ctx.enter_context(nc.psum_tensor(name, shape, dt))

        sems = []

        def sem(name):
            s = ctx.enter_context(nc.semaphore(name))
            sems.append(s)
            return s

        wq_sb = sb("wq_sb", [P, INNER])
        wkv_sb = sb("wkv_sb", [P, 2 * DH])
        wout_sb = sb("wout_sb", [P, INNER // P, D])
        router_sb = sb("router_sb", [E, D])
        routerT = sb("routerT", [P, E])
        g_col = sb("g_col", [P, 1])
        outg_row = sb("outg_row", [P, D])
        c_T = sb("c_T", [P, NB])
        silu_T = sb("silu_T", [P, NB])
        wmod_sb = sb("wmod_sb", [P, 6 * D])
        mod = sb("mod", [P, NB, 6, D])
        ident = sb("ident", [P, P])
        ident16 = sb("ident16", [P, P], F16)
        tick = sb("tick", [P, 1])
        power = sb("power", [P, 16])
        clamp = sb("clamp", [P, NQK])
        rows_a = sb("rows_a", [P, 2, D])
        rows_f = sb("rows_f", [P, 3, D])
        x_in = sb("x_in", [P, D])
        xn_a = sb("xn_a", [P, D])
        hs_a = sb("hs_a", [P, D])
        h_a = sb("h_a", [P, D])
        xhat = sb("xhat", [P, D])
        st_1, st_2 = sb("st_1", [P, 2, 6]), sb("st_2", [P, 2, 6])
        mv_1, mv_2 = sb("mv_1", [P, 2, 2]), sb("mv_2", [P, 2, 2])
        ve_1, ve_2 = sb("ve_1", [P, 2]), sb("ve_2", [P, 2])
        rs_1, rs_2 = sb("rs_1", [P, 2]), sb("rs_2", [P, 2])
        xnT = sb("xnT", [P, P])
        qkv = sb("qkv", [P, INNER + 2 * DH])
        sq = sb("sq", [P, NQK * DH])
        ss = sb("ss", [P, NQK])
        z = sb("z", [P, NQK])
        rq = sb("rq", [P, NQK])
        qn = sb("qn", [P, NQK * DH])
        qs = sb("qs", [P, NQK + 1, 2 * DH], F16)
        q_next = sb("q_next", [P, H, HALF], F16)
        q_cur = sb("q_cur", [P, 2, H, HALF], F16)
        k_next = sb("k_next", [P, 2, N], F16)
        k_cur = sb("k_cur", [P, 2, N], F16)
        v_next = sb("v_next", [P, TB, VP], BF16)
        v_cur = sb("v_cur", [P, TB, VP], BF16)
        probs = sb("probs", [P, RING, 2 * HALF])
        rest = sb("rest", [P, RING, 2 * HALF], BF16)
        o_raw = sb("o_raw", [P, 2, HT, VC])
        silu_b = o_raw[:].rearrange("p a t c -> p (a t c)")[:, 0:NB * P].rearrange("p (b n) -> p b n", b=NB)
        gmag = probs[:].rearrange("p r n -> p (r n)")[:, 0:NB * 4 * D].rearrange("p (b k d) -> p b k d", b=NB, k=4)
        o_rin = sb("o_rin", [P, 2, HT])
        o_sum = sb("o_sum", [P, HT, DH])
        o_all = sb("o_all", [P, 2, HT, INNER])
        oT = sb("oT", [P, INNER // P, P])
        y_o = sb("y_o", [P, D])
        x_res = sb("x_res", [P, D])
        yn = sb("yn", [P, D])
        yg = sb("yg", [P, D])
        pay = sb("pay", [P, 4, W])
        hn = sb("hn", [P, D])
        hc = sb("hc", [P, D])
        h2T = sb("h2T", [P, P])
        lg = sb("lg", [P, E])
        first_pref = sb("first_pref", [P, E])
        e_base = sb("e_base", [P, E])
        below = sb("below", [P, P], BF16)
        ones16 = sb("ones16", [P, P], BF16)
        lg_max = sb("lg_max", [P, 1])
        lg_eq = sb("lg_eq", [P, E])
        eq_max = sb("eq_max", [P, 1])
        chosen = sb("chosen", [P, E])
        chosen16 = sb("chosen16", [P, E], BF16)
        counted = sb("counted", [P, E], BF16)
        place = sb("place", [P, E])
        place_c = sb("place_c", [P, E])
        dest = sb("dest", [P, 1])
        dest_i = sb("dest_i", [P, 4, 1], U32)
        filler = sb("filler", [P, W])
        p_tick = sb("p_tick", [P, 1])
        fc_sb = sb("fc_sb", [P, E, HID])
        fc_lo = sb("fc_lo", [P, E, HID], BF16)
        pjT = sb("pjT", [P, E, HC, D])
        pj_hl = sb("pj_hl", [P, E, HC, 2, D], BF16)
        pj_in = o_all[:].rearrange("p a t i -> p (a t i)").rearrange("p (e h) -> p e h", e=E)
        blk_i = sb("blk_i", [P, NBLK], I32)
        blk = sb("blk", [P, NBLK])
        part_i = sb("part_i", [P, 1], I32)
        part = sb("part", [P, 1])
        total = sb("total", [P, E])
        total_i = sb("total_i", [P, E], I32)
        nblk = sb("nblk", [P, E])
        start = sb("start", [P, E + 1])
        jump = sb("jump", [P, E])
        free = o_all[:].rearrange("p a t i -> p (a t i)")
        past = free[:, 0:E * NBLK].rearrange("p (e j) -> p e j", e=E)
        past_j = free[:, E * NBLK:2 * E * NBLK].rearrange("p (e j) -> p e j", e=E)
        relu = free[:, 4 * HID:6 * HID].rearrange("p (k h) -> p k h", k=2)
        act2 = free[:, 6 * HID:8 * HID].rearrange("p (k h) -> p k h", k=2)
        row_f = sb("row_f", [P, NBLK])
        exp_f = sb("exp_f", [P, NBLK])
        row_tab = sb("row_tab", [P, NBLK], I32)
        digit = sb("digit", [P, NBLK // WORD, WORD])
        word_f = sb("word_f", [P, NBLK // WORD])
        exp_tab = sb("exp_tab", [P, NBLK // WORD], I32)
        fill_i = sb("fill_i", [P, E], I32)
        free = probs[:].rearrange("p r n -> p (r n)")
        b_in = free[:, 0:BR * W].rearrange("p (k w) -> p k w", k=BR)
        act2_lo = rest[:].rearrange("p r n -> p (r n)")[:, 0:2 * HID].rearrange("p (k h) -> p k h", k=2)
        hT = sb("hT", [P, 2, P])
        hT_lo = sb("hT_lo", [P, 2, P], BF16)
        y_s = sq[:, 0:2 * D].rearrange("p (k d) -> p k d", k=2)
        y_g = sq[:, 2 * D:4 * D].rearrange("p (k d) -> p k d", k=2)
        y_fin = qkv[:, 0:4 * D].rearrange("p (k d) -> p k d", k=4)
        tok_i = sb("tok_i", [P, 4, 1], U32)

        ps_s = pb("ps_s", [P, 2, 2, HALF])
        ps_o = pb("ps_o", [P, 2, 512])
        ps_m0 = pb("ps_m0", [P, 512])
        ps_m1 = pb("ps_m1", [P, 512])
        ps_m0h = ps_m0[:].bitcast(F16)
        ps_m1h = ps_m1[:].bitcast(F16)
        ps_o0h = ps_o[:, 0, :].bitcast(F16)
        ps_o1h = ps_o[:, 1, :].bitcast(F16)

        s_c = sem("conditioning_loaded")
        s_wm = sem("wmod_loaded")
        s_w = sem("weights_loaded")
        s_id = sem("identity_steps")
        s_const = sem("constants_ready")
        s_silu = sem("silu_steps")
        s_silub = sem("silu_broadcast")
        s_modmm = sem("mod_products")
        s_modcp = sem("mod_copied")
        s_modf = sem("mod_finishing")
        s_mod1 = sem("ca_plus_one")
        s_modr = sem("mod_ready")
        s_rT = sem("router_transposed")
        s_rowa = sem("rows_a_moved")
        s_rowf = sem("rows_f_moved")
        s_tick = sem("waited")
        s_xin = sem("x_in_loaded")
        s_xres = sem("x_res_loaded")
        s_scores = sem("scores_ready")
        s_exp = sem("exp_done")
        s_rest = sem("rest_ready")
        s_pv = sem("pv_done")
        s_ocp = sem("o_copied")
        s_orin = sem("o_reciprocal")
        s_osum = sem("o_summed")
        s_onorm = sem("o_normed")
        s_kst = sem("k_staged")
        s_vst = sem("v_staged")
        s_qst = sem("q_staged")
        s_kcur = sem("k_moved")
        s_vcur = sem("v_moved")
        s_qcur = sem("q_moved")
        s_ones = sem("ones_set")
        s_ja = sem("xhat_transposed")
        s_xnT = sem("xnT_ready")
        s_jq = sem("q_projected")
        s_jkv = sem("kv_projected")
        s_qcp = sem("q_copied")
        s_kvcp = sem("kv_copied")
        s_jqT = sem("q_transposed")
        s_jkT = sem("k_transposed")
        s_jo = sem("o_transposed")
        s_oT = sem("oT_ready")
        s_jy = sem("y_projected")
        s_y = sem("y_copied")
        s_jh = sem("h2_transposed")
        s_h2T = sem("h2T_ready")
        s_jl = sem("logits_product")
        s_lg = sem("logits_copied")
        s_v1 = sem("variances_1")
        s_r1 = sem("rsqrt_1")
        s_v2 = sem("variances_2")
        s_r2 = sem("rsqrt_2")
        s_xa = sem("xn_a_ready")
        s_ha = sem("h_a_steps")
        s_xh = sem("xhat_ready")
        s_sq = sem("squares_ready")
        s_ss = sem("norms_squared")
        s_rq = sem("rsqrt_q")
        s_qn = sem("qn_ready")
        s_hi = sem("q_hi_ready")
        s_vhi = sem("v_hi_ready")
        s_lo = sem("q_lo_ready")
        s_yn = sem("yn_ready")
        s_x1 = sem("x1_steps")
        s_hn = sem("hn_ready")
        s_h2 = sem("h2_steps")
        s_pw = sem("proj_loaded")
        s_fw = sem("fc_loaded")
        s_pj = sem("proj_transposed")
        s_wlo = sem("low_weights_ready")
        s_pjc = sem("proj_copied")
        s_rc0 = sem("routing_constants")
        s_tok = sem("token_numbers")
        s_rt = sem("choice_steps")
        s_jr = sem("ranks_product")
        s_pl = sem("place_steps")
        s_cnt = sem("counted")
        s_sc = [sem(f"rows_scattered_{k}") for k in range(4)]
        s_ptick = sem("pool_waited")
        f_tot = sem("totals_product")
        f_map = sem("block_map_steps")
        f_fill = sem("blocks_filled")
        f_none = sem("nobodys_block_written")
        f_ld = [sem(f"block_loaded_{k}") for k in range(BR)]
        f_T = sem("block_transposed")
        f_hT = sem("block_hT_copied")
        f_hL = sem("block_hT_lo")
        f_F = sem("up_product")
        f_rl = sem("relu_done")
        f_sq = sem("squared")
        f_gL = sem("act2_lo_ready")
        f_D = sem("down_product")
        f_ys = sem("y_summed")
        f_yg = sem("y_gated")
        f_yf = sem("y_finished")
        f_sc = [sem(f"out_scattered_{k}") for k in range(4)]

        def wait(eng, s, v):
            if not isinstance(v, int) or v > 0:
                eng.wait_ge(s, v)

        def known(v, lo, hi):
            return not isinstance(v, int) or lo <= v < hi

        def cols(ta, rp):
            have = [known(ta, 0, NT), known(rp, 0, NT)]
            return slice(0 if have[0] else 1, 2 if have[1] else 1) if any(have) else None

        def sweep(eng, macro):
            for m in range(TB):
                macro(0, m)
            with eng.Fori(1, NB - 1) as b:
                for m in range(TB):
                    macro(b, m)
            for m in range(TB):
                macro(NB - 1, m)
            for m in range(HT + 3):
                macro(NB, m)

        M0_JOBS = [(0, 7, s_qst, 1), (1, 8, s_xnT, 1), (3, 8, s_qcp, 1), (4, -6, s_pl, 3), (6, -4, s_y, 1),
                   (7, -5, s_lg, 1)]
        M1_JOBS = [(0, 7, s_kst, 1), (3, 8, s_kvcp, 1), (4, -4, s_oT, 1), (6, -5, s_h2T, 1)]

        def bank_free(pe, jobs, b, m, slot):
            M = b * TB + m
            if isinstance(b, int):
                for s, o, sm, per in jobs:
                    wait(pe, sm, per * max(0, min(M + o + (s < slot), NT)))
            else:
                s, o, sm, per = ([j for j in jobs if j[0] < slot] or jobs)[-1]
                wait(pe, sm, per * (M + o + (s < slot)))

        def after_last(b):
            return isinstance(b, int) and b == NB

        def y_slot(b):
            return 4 if after_last(b) else 6

        def y_bank(b):
            return ps_s[:, 0, 0, 0:D] if after_last(b) else ps_m0[:, 0:D]

        def rows_of(b, k0, k1, off=0):
            if isinstance(b, int):
                return mod[:, (b + off) % NB, k0:k1, :]
            return mod[:, bass.ds((b + off) % NB if off else b, 1), k0:k1, :].rearrange("p o k d -> p (o k) d")

        def gate_of(b):
            if isinstance(b, int):
                return mod[:, b, 5, :]
            return mod[:, bass.ds(b, 1), 5, :].rearrange("p o d -> p (o d)")

        def top(ap):
            return ap.bitcast(BF16).rearrange("p (n two) -> p n two", two=2)[:, :, 1]

        def tile_of(ap, b, k):
            if isinstance(b, int):
                return ap[TB * b + k]
            return ap[bass.ds(b * TB + k, 1)].rearrange("o p d -> (o p) d")

        MAP_STEPS = 17 + E
        FILL_STEPS = 2

        def run_blocks(eng, *stages, group=None):
            group = group or (lambda j: None)
            most = max(ahead for _, ahead in stages)

            def turn(j, k):
                for f, ahead in stages:
                    if isinstance(j, int) and not 0 <= j + ahead < NBLK:
                        continue
                    f(j + ahead, (k + ahead) % BR)
            group(0)
            for j in range(-most, BR):
                turn(j, j % BR)
            with eng.Fori(1, NBLK // BR - 1) as i:
                group(i * BR)
                for k in range(BR):
                    turn(BR * i + k, k)
            group(NBLK - BR)
            for k in range(BR):
                turn(NBLK - BR + k, k)

        block = ctx.enter_context(nc.Block())

        @block.sync
        def _(sp):
            loads = [
                (g_col[:], norm_g.rearrange("(d o) -> d o", o=1)),
                (wq_sb[:], wq), (wkv_sb[:], wkv),
                (wout_sb[:], wout.rearrange("(j p) n -> p j n", p=P)),
                (router_sb[:], router),
                (outg_row[:], out_g.rearrange("(o d) -> o d", o=1).broadcast_to([P, D])),
            ]
            sp.dma_start(c_T[:], c).then_inc(s_c, 16)
            sp.dma_start(wmod_sb[:], wmod).then_inc(s_wm, 16)
            sp.dma_start(x_in[:], x_t[0]).then_inc(s_xin, 16)
            for dst, src in loads:
                sp.dma_start(dst, src).then_inc(s_w, 16)

            def macro(b, m):
                M = b * TB + m
                t = M + 9
                if known(t, 1, NT):
                    wait(sp, s_xa, t)
                    if isinstance(b, int):
                        src = x_t[t]
                    elif m == TB - 1:
                        src = x_t[bass.ds(((b + 2) % NB) * TB, 1)].rearrange("o p d -> (o p) d")
                    else:
                        src = tile_of(x_t, b, m + 9)
                    sp.dma_start(x_in[:], src).then_inc(s_xin, 16)
                r = M - 4
                if known(r, 0, NT):
                    wait(sp, s_x1, 2 * r)
                    sp.dma_start(x_res[:], tile_of(x_t, b, m - 4)).then_inc(s_xres, 16)

            for m in range(TB):
                macro(-1, m)
                if m == 0:
                    sp.dma_start(pj_in, proj.rearrange("e d h -> d e h")).then_inc(s_pw, 16)
                if m == 2:
                    sp.dma_start(fc_sb[:], fc.rearrange("e d h -> d e h")).then_inc(s_fw, 16)
            sweep(sp, macro)

            def load(j, k):
                wait(sp, f_yf, j + 1 - BR)
                base = sp.value_load(row_tab[0:1, bass.ds(j, 1)] if not isinstance(j, int) else row_tab[0:1, j:j + 1],
                                     min_val=0, max_val=E * CAP)
                sp.dma_start(b_in[:, k, :], rows_dram[bass.ds(base, P), :]).then_inc(f_ld[k], 16)

            sp.wait_ge(f_map, FILL_STEPS)
            ends = nc.values_load_multi_w_load_instructions(
                fill_i[0:1, :], engines=[mybir.EngineType.SP], min_val=0, max_val=E * CAP - P)[1]
            for e in range(E):
                sp.dma_start(rows_dram[bass.ds(ends[e], P), :], filler[:]).then_inc(f_fill, 16)
            sp.wait_ge(f_map, MAP_STEPS)
            for k in range(4):
                sp.wait_ge(s_sc[k], 4 * NT)
            sp.wait_ge(f_none, 16)
            sp.wait_ge(f_fill, 16 * E)
            for k in range(BR):
                load(k, k)
            with sp.Fori(1, NBLK // BR) as i:
                for k in range(BR):
                    load(BR * i + k, k)
            for k in range(4):
                sp.wait_ge(f_sc[k], 4 * NBLK)

        @block.gpsimd
        def _(pool):
            g = nc.gpsimd
            g.memset(ident[:], 0.0).then_inc(s_id, 1)
            g.memset(power[:], -0.5)
            g.memset(clamp[:, 0:H], 1e-24 / SCALE ** 2 / 16.0)
            g.memset(clamp[:, H:NQK], 1e-24 / 16.0).then_inc(s_id, 1)
            pool.wait_ge(s_id, 2)
            g.affine_select(out=ident[:], in_=ident[:], compare_op=ALU.not_equal, fill=1.0, base=0,
                            pattern=[[-1, P]], channel_multiplier=1).then_inc(s_id, 1)
            pool.wait_ge(s_id, 3)
            g.tensor_copy(ident16[:], ident[:]).then_inc(s_const, 1)
            for e in range(E):
                g.memset(first_pref[:, e:e + 1], float(E - e))
                g.memset(e_base[:, e:e + 1], float(e * CAP))
            for k in range(WORD):
                g.memset(digit[:, :, k], float(E ** k))
            g.memset(below[:], 1.0).then_inc(s_rc0, 1)
            g.memset(ones16[:], 1.0)
            g.memset(counted[:], 0.0)
            g.memset(pay[:], 0.0)
            g.memset(p_tick[:], 0.0)
            g.iota(part_i[:], pattern=[[0, 1]], base=0, channel_multiplier=1)
            g.iota(blk_i[:], pattern=[[1, NBLK]], base=0, channel_multiplier=0)
            g.memset(filler[:], 0.0).then_inc(s_rc0, 1)
            pool.wait_ge(s_rc0, 2)
            g.affine_select(out=below[:], in_=below[:], compare_op=ALU.is_gt, fill=0.0, base=0,
                            pattern=[[1, P]], channel_multiplier=-1)
            g.memset(filler[:, TOK:TOK + 1], NOBODY).then_inc(s_rc0, 1)
            g.memset(v_next[:], 1.0).then_inc(s_ones, 1)
            g.memset(v_cur[:], 1.0).then_inc(s_ones, 1)
            pool.wait_ge(s_ones, 2)

            def scatter(dst, idx, src, **bounds):
                return g.indirect_dma_start(dst, bass.IndirectOffsetOnAxis(ap=idx, axis=0), src, None, **bounds)

            def send_rows(q, k):
                wait(pool, s_pl, 3 * (q + 1))
                wait(pool, s_tok, q + 1)
                wait(pool, s_ptick, q)
                g.tensor_tensor(p_tick[:], p_tick[:], p_tick[:], ALU.add).then_inc(s_ptick, 1)
                scatter(rows_dram, dest_i[:, k, :], pay[:, k, :]).then_inc(s_sc[k], 16)

            def rsqrt_qk(t):
                wait(pool, s_ss, 2 * (t + 1))
                g.tensor_tensor(rq[:], z[:], power[:, 0:NQK], ALU.pow).then_inc(s_rq, 1)

            def macro(b, m):
                M = b * TB + m
                ta, t, r, rp = M + 9, M + 8, M - 4, M - 5
                both = cols(ta, rp)
                if both:
                    wait(pool, s_v1, 3 * (M + 10))
                    g.tensor_tensor(rs_1[:, both], ve_1[:, both], power[:, both], ALU.pow).then_inc(s_r1, 1)

                def norm_o(u, free):
                    wait(pool, s_ocp, u + 1)
                    wait(pool, s_onorm, u)
                    raw = o_raw[:, um, :, :]
                    g.tensor_tensor(o_sum[:], raw[:, :, 0:DH], raw[:, :, DH:2 * DH], ALU.add).then_inc(s_osum, 1)
                    wait(pool, s_osum, u + 1)
                    wait(pool, s_orin, u + 1)
                    if free is not None:
                        wait(pool, s_jo, free)
                    g.tensor_tensor(o_all[:, uh, :, hh * DH:(hh + 1) * DH], o_sum[:],
                                    o_rin[:, um, :].rearrange("p (t o) -> p t o", o=1).broadcast_to([P, HT, DH]),
                                    ALU.mult).then_inc(s_onorm, 1)

                if known(ta, 0, NT):
                    wait(pool, s_xa, ta + 1)
                    if m == TB - 1:
                        wait(pool, s_rowa, b + 3)
                    g.tensor_tensor(hs_a[:], xn_a[:], rows_a[:, 1, :], ALU.mult).then_inc(s_ha, 1)
                    wait(pool, s_ha, 2 * ta + 1)
                    g.tensor_tensor(h_a[:], hs_a[:], rows_a[:, 0, :], ALU.add).then_inc(s_ha, 1)
                if known(rp, 0, NT):
                    wait(pool, s_yn, rp + 1)
                    if m == 5:
                        wait(pool, s_rowf, b + 1)
                    g.tensor_tensor(yg[:], yn[:], rows_f[:, 0, :], ALU.mult).then_inc(s_x1, 1)
                    wait(pool, s_x1, 2 * rp + 1)
                    wait(pool, s_xres, 16 * (rp + 1))
                    k = (m - 5) % 4
                    wait(pool, s_sc[k], 4 * (rp - k))
                    g.tensor_tensor(pay[:, (m - 5) % 4, D:2 * D], yg[:], x_res[:], ALU.add).then_inc(s_x1, 1)
                if known(M - 1, 0, NT):
                    mm = (m - 1) % TB
                    um, uh, hh = 1, mm // 4, 2 * (mm % 4) + 1
                    norm_o(2 * M - 1, None)
                if after_last(b) and m > 0:
                    send_rows(M - 7, (m - 7) % 4)
                if both:
                    wait(pool, s_v2, 3 * (M + 10))
                    g.tensor_tensor(rs_2[:, both], ve_2[:, both], power[:, both], ALU.pow).then_inc(s_r2, 1)
                if known(rp, 0, NT):
                    wait(pool, s_hn, rp + 1)
                    g.tensor_tensor(hc[:], hn[:], rows_f[:, 2, :], ALU.mult).then_inc(s_h2, 1)
                    wait(pool, s_h2, 2 * rp + 1)
                    g.tensor_tensor(pay[:, (m - 5) % 4, 0:D], hc[:], rows_f[:, 1, :], ALU.add).then_inc(s_h2, 1)
                if known(t, 0, NT):
                    rsqrt_qk(t)
                if known(M, 0, NT):
                    um, uh, hh = 0, m // 4, 2 * (m % 4)
                    norm_o(2 * M, 4 * (M // 4 - 1) if isinstance(b, int) and m % 4 == 0
                           else (8 * b + 4 * (m // 4 - 1) if m % 4 == 0 else None))
                if known(M - 6, 0, NT) and not after_last(b):
                    send_rows(M - 6, (m - 6) % 4)
                if isinstance(b, int) and b == 0:
                    wait(pool, s_fw, 16)
                    g.tensor_tensor(fc_lo[:, m, :], fc_sb[:, m, :], top(fc_sb[:, m, :]), ALU.subtract).then_inc(s_wlo, 1)
                    wait(pool, s_pjc, m + 1)
                    hi = pjT[:, m, :, :].bitcast(BF16).rearrange("p j (d two) -> p j d two", two=2)[:, :, :, 1]
                    g.tensor_copy(pj_hl[:, m, :, 0, :], hi)
                    g.tensor_tensor(pj_hl[:, m, :, 1, :], pjT[:, m, :, :], hi, ALU.subtract).then_inc(s_wlo, 1)

            def first_norm(a):
                pool.wait_ge(s_v1, 3 * (a + 1))
                g.tensor_tensor(rs_1[:, 0:1], ve_1[:, 0:1], power[:, 0:1], ALU.pow).then_inc(s_r1, 1)
                pool.wait_ge(s_xa, a + 1)
                pool.wait_ge(s_rowa, 1 + a // TB)
                g.tensor_tensor(hs_a[:], xn_a[:], rows_a[:, 1, :], ALU.mult).then_inc(s_ha, 1)
                pool.wait_ge(s_ha, 2 * a + 1)
                g.tensor_tensor(h_a[:], hs_a[:], rows_a[:, 0, :], ALU.add).then_inc(s_ha, 1)

            def second_norm(a):
                pool.wait_ge(s_v2, 3 * (a + 1))
                g.tensor_tensor(rs_2[:, 0:1], ve_2[:, 0:1], power[:, 0:1], ALU.pow).then_inc(s_r2, 1)

            for a in range(2):
                first_norm(a)
                second_norm(a)
            for t in range(TB):
                if t + 2 <= TB:
                    first_norm(t + 2)
                rsqrt_qk(t)
                if t + 2 <= TB:
                    second_norm(t + 2)
            pool.wait_ge(s_rc0, 3)
            pool.dma_start(rows_dram[E * CAP:E * CAP + P, :], filler[:]).then_inc(f_none, 16)
            sweep(pool, macro)

            def finish(j, k):
                wait(pool, f_yf, j + 1)
                wait(pool, s_ptick, NT + j)
                g.tensor_tensor(p_tick[:], p_tick[:], p_tick[:], ALU.add).then_inc(s_ptick, 1)
                scatter(out_rows, tok_i[:, k % 4, :], y_fin[:, k % 4, :], bounds_check=NTOK - 1, oob_is_err=False
                        ).then_inc(f_sc[k % 4], 16)

            run_blocks(pool, (finish, 0))

        @block.scalar
        def _(act):
            a = nc.scalar
            act.wait_ge(s_c, 16)
            a.activation(silu_T[:], c_T[:], ACT.Exp, scale=-1.0).then_inc(s_silu, 1)
            for b in range(NB):
                act.wait_ge(s_modmm, b + 1)
                a.copy(mod[:, b, 0:3, :], ps_s[:, b % 2, 0, 0:3 * D].rearrange("p (k d) -> p k d", k=3))
                a.copy(mod[:, b, 3:6, :], ps_s[:, b % 2, 1, 0:3 * D].rearrange("p (k d) -> p k d", k=3)
                       ).then_inc(s_modcp, 1)
            act.wait_ge(s_rT, 1)
            a.copy(routerT[:], ps_m0[:, 0:E]).then_inc(s_modcp, 1)

            def copy_qkT(tp, qm, q_free, k_free, psq, psk):
                wait(act, s_jkT, tp + 1)
                wait(act, s_kcur, k_free)
                a.copy(k_next[:, :, qm * P:(qm + 1) * P],
                       psk[:, 0:2 * P].rearrange("p (h n) -> p h n", h=2)).then_inc(s_kst, 1)
                wait(act, s_jqT, tp + 1)
                wait(act, s_qcur, q_free)
                a.copy(q_next[:, :, (qm % HT) * P:(qm % HT + 1) * P],
                       psq[:, 0:H * P].rearrange("p (h n) -> p h n", h=H)).then_inc(s_qst, 1)

            def copy_xnT(t):
                wait(act, s_ja, t + 1)
                wait(act, s_jkv, t)
                a.activation(xnT[:], ps_m0[:, 0:P], ACT.Copy, scale=g_col[:, 0:1]).then_inc(s_xnT, 1)

            def copy_qkv(t, m, v_free):
                wait(act, s_jq, t + 1)
                wait(act, s_qn, t)
                a.copy(qkv[:, 0:INNER], ps_m0[:, 0:INNER]).then_inc(s_qcp, 1)
                wait(act, s_jkv, t + 1)
                wait(act, s_vst, t)
                a.copy(qkv[:, INNER:INNER + 2 * DH], ps_m1[:, 0:2 * DH]).then_inc(s_kvcp, 1)
                wait(act, s_qcp, t + 1)
                wait(act, s_kvcp, t + 1)
                wait(act, s_ss, 2 * t)
                a.activation(sq[:], qkv[:, 0:NQK * DH], ACT.Square).then_inc(s_sq, 1)
                wait(act, s_vcur, v_free)
                wait(act, s_ones, 1)
                a.copy(v_next[:, m, 0:DH], qkv[:, NQK * DH:(NQK + 1) * DH]).then_inc(s_vhi, 1)

            def high_parts(t):
                wait(act, s_qn, t + 1)
                wait(act, s_jqT, t)
                wait(act, s_jkT, t)
                qn3 = qn[:].rearrange("p (h d) -> p h d", d=DH)
                a.copy(qs[:, 0:NQK, 0:DH], qn3)
                a.copy(qs[:, H, DH:2 * DH], qn3[:, H, :]).then_inc(s_hi, 1)

            def exp_scores(X, k):
                wait(act, s_scores, X + LOOK + 1)
                wait(act, s_pv, X + LOOK - RING + 1)
                a.activation(probs[:, k % RING, :], ps_s[:, k % 2, :, :].rearrange("p k n -> p (k n)"),
                             ACT.Exp).then_inc(s_exp, 1)

            def copy_proj(e):
                wait(act, s_pj, e + 1)
                a.copy(pjT[:, e, :, :], ps_s[:, e % 2, 0, :].rearrange("p (j d) -> p j d", j=HC)).then_inc(s_pjc, 1)

            act.wait_ge(s_w, 16 * 6)
            copy_xnT(0)
            for t in range(TB + 1):
                if t < TB:
                    copy_qkv(t, t, 0)
                if t + 1 < TB:
                    copy_xnT(t + 1)
                if t >= 1:
                    high_parts(t - 1)
                if t >= 2:
                    copy_qkT(t - 2, t - 2, (t - 2) // HT, 0, ps_o0h, ps_o1h)
                if t >= 1:
                    copy_proj(t - 1)
            act.wait_ge(s_modr, 1)
            for k in range(LOOK):
                exp_scores(k - LOOK, k)

            def macro(b, m):
                M = b * TB + m
                t, tp, r, rp = M + 8, M + 7, M - 4, M - 5
                for s in range(NS):
                    X = M * NS + s
                    if s in (1, 5):
                        U = 2 * M - 1 if s == 1 else 2 * M
                        if known(M - (s == 1), 0, NT):
                            wait(act, s_pv, 4 * (U + 1))
                            wait(act, s_onorm, U - 1)
                            par = 1 if s == 1 else 0
                            a.copy(o_raw[:, par, :, :].rearrange("p (k t) d -> p k (t d)", k=2),
                                   ps_o[:, :, 0:2 * VC]).then_inc(s_ocp, 1)
                    if s == 0 and known(tp, 0, NT):
                        qm = (m - 1) % TB
                        copy_qkT(tp, qm, 2 * b + 2 + (1 if m > 4 else 0) if m > 0 else 2 * b + 1,
                                 4 * b + qm // 2 + 1 if m > 0 else 4 * (b - 1) + qm // 2 + 1, ps_m0h, ps_m1h)
                    if s == 1 and known(t, 0, NT):
                        copy_xnT(t)
                    if s == 3 and known(t, 0, NT):
                        copy_qkv(t, m, 4 * b + m // 2 + 1)
                    if s == 4 and known(r, 0, NT):
                        wait(act, s_jo, r + 1)
                        wait(act, s_jy, r)
                        a.copy(oT[:], ps_m1[:].rearrange("p (j n) -> p j n", n=P)).then_inc(s_oT, 1)
                    if s == 6 and known(r, 0, NT):
                        wait(act, s_jy, r + 1)
                        wait(act, s_yn, r)
                        a.copy(y_o[:], y_bank(b)).then_inc(s_y, 1)
                    if s == 6 and known(rp, 0, NT):
                        wait(act, s_jh, rp + 1)
                        wait(act, s_jl, rp)
                        a.copy(h2T[:], ps_m1[:, 0:P]).then_inc(s_h2T, 1)
                    if s == 7 and known(t, 0, NT):
                        high_parts(t)
                    if s == 7 and known(rp, 0, NT):
                        wait(act, s_jl, rp + 1)
                        wait(act, s_rt, 4 * rp)
                        a.copy(lg[:], ps_m0[:, 0:E]).then_inc(s_lg, 1)
                    if known(X + LOOK, 0, NT * NS):
                        exp_scores(X, (s + LOOK) % NS)

            sweep(act, macro)

            def copy_hT(j, k):
                wait(act, f_T, j + 1)
                wait(act, f_F, j - 1)
                wait(act, f_hL, j - 1)
                a.copy(hT[:, k % 2, :], ps_o[:, k % 2, 0:P]).then_inc(f_hT, 1)

            def do_relu(j, k):
                wait(act, f_F, j + 1)
                wait(act, f_sq, j - 1)
                a.activation(relu[:, k % 2, :], ps_s[:, 0, k % 2, :], ACT.Relu).then_inc(f_rl, 1)

            def square(j, k):
                wait(act, f_rl, j + 1)
                wait(act, f_D, j - 1)
                wait(act, f_gL, j - 1)
                a.activation(act2[:, k % 2, :], relu[:, k % 2, :], ACT.Square).then_inc(f_sq, 1)

            run_blocks(act, (copy_hT, 3), (do_relu, UP_AHEAD), (square, UP_AHEAD))

        @block.vector
        def _(dve):
            v = nc.vector
            dve.wait_ge(s_silu, 1)
            v.tensor_scalar_add(silu_T[:], silu_T[:], 1.0).then_inc(s_silu, 1)
            dve.wait_ge(s_silu, 2)
            v.reciprocal(silu_T[:], silu_T[:]).then_inc(s_silu, 1)
            dve.wait_ge(s_silu, 3)
            v.tensor_tensor(silu_T[:], silu_T[:], c_T[:], ALU.mult).then_inc(s_silu, 1)
            dve.wait_ge(s_silu, 4)
            v.tensor_copy(silu_b, silu_T[:].rearrange("p (b o) -> p b o", o=1).broadcast_to([P, NB, P])
                          ).then_inc(s_silub, 1)

            def gate_step(i):
                wait(dve, s_modf, 2 * i)
                for j, k in ((0, 2), (1, 5)):
                    gm, gs, g_in = gmag[:, :, 2 * j, :], gmag[:, :, 2 * j + 1, :], mod[:, :, k, :]
                    if i == 0:
                        v.tensor_scalar(gm, g_in, -1.0, 0.25, ALU.mult, ALU.max).then_inc(s_modf, 1)
                    if i == 1:
                        v.tensor_tensor(gm, gm, g_in, ALU.max).then_inc(s_modf, 1)
                    if i == 2:
                        v.tensor_scalar(gs, g_in, 0.0, 2.0, ALU.is_ge, ALU.mult).then_inc(s_modf, 1)
                    if i == 3:
                        v.tensor_scalar_add(gs, gs, -1.0).then_inc(s_modf, 1)
                    if i == 4:
                        v.tensor_tensor(g_in, gm, gs, ALU.mult).then_inc(s_modf, 1)
                if i == 5:
                    v.tensor_tensor(mod[:, :, 2, :], mod[:, :, 2, :],
                                    outg_row[:].rearrange("p (o d) -> p o d", o=1).broadcast_to([P, NB, D]),
                                    ALU.mult)
                    v.tensor_scalar_add(mod[:, :, 4, :], mod[:, :, 4, :], 1.0).then_inc(s_modr, 1)

            def stats(srcs, both, st, mv, ve, chain, i):
                for k, src in srcs:
                    last = v.bn_stats(st[:, k, :], src)
                last.then_inc(chain, 1)
                wait(dve, chain, 3 * i + 1)
                v.tensor_scalar_add(tick[:], power[:, 0:1], 1.0)
                for k, src in srcs:
                    last = v.bn_aggr(mv[:, k, :], st[:, k, :])
                last.then_inc(chain, 1)
                wait(dve, chain, 3 * i + 2)
                v.tensor_scalar_add(ve[:, both], mv[:, both, 1], EPS).then_inc(chain, 1)

            def normed(dst, src, mv, rs, k, done):
                v.tensor_scalar(dst[:], src, mv[:, k, 0:1], rs[:, k:k + 1], ALU.subtract, ALU.mult).then_inc(done, 1)

            def x1_of(m):
                return pay[:, (m - 5) % 4, D:2 * D]

            def stats_1(i, a, c):
                srcs = []
                if known(a, 0, NT):
                    wait(dve, s_xin, 16 * (a + 1))
                    srcs.append((0, x_in[:]))
                if known(c, 0, NT):
                    wait(dve, s_y, c + 1)
                    srcs.append((1, y_o[:]))
                stats(srcs, cols(a, c), st_1, mv_1, ve_1, s_v1, i)

            def stats_2(i, a, c, m):
                srcs = []
                if known(a, 0, NT):
                    wait(dve, s_ha, 2 * (a + 1))
                    srcs.append((0, h_a[:]))
                if known(c, 0, NT):
                    wait(dve, s_x1, 2 * (c + 1))
                    srcs.append((1, x1_of(m)))
                stats(srcs, cols(a, c), st_2, mv_2, ve_2, s_v2, i)

            def norm_1(i, a, c):
                wait(dve, s_r1, i + 1)
                wait(dve, s_v1, 3 * (i + 1))
                if known(a, 0, NT):
                    wait(dve, s_ha, 2 * a)
                    normed(xn_a, x_in[:], mv_1, rs_1, 0, s_xa)
                if known(c, 0, NT):
                    wait(dve, s_x1, 2 * c)
                    normed(yn, y_o[:], mv_1, rs_1, 1, s_yn)

            def norm_2(i, a, c, m):
                wait(dve, s_r2, i + 1)
                wait(dve, s_v2, 3 * (i + 1))
                if known(a, 0, NT):
                    wait(dve, s_ja, a)
                    normed(xhat, h_a[:], mv_2, rs_2, 0, s_xh)
                if known(c, 0, NT):
                    wait(dve, s_h2, 2 * c)
                    normed(hn, x1_of(m), mv_2, rs_2, 1, s_hn)

            dve.wait_ge(s_rc0, 3)
            v.tensor_copy(blk[:], blk_i[:])
            v.tensor_copy(part[:], part_i[:]).then_inc(s_rc0, 1)
            dve.wait_ge(s_rc0, 4)
            for k in range(4):
                last = v.tensor_scalar_add(pay[:, k, TOK:TOK + 1], part[:], float((k if k < 3 else -1) * P))
            last.then_inc(s_rc0, 1)
            dve.wait_ge(s_rc0, 5)
            dve.wait_ge(s_const, 1)

            def squared_norms(t):
                wait(dve, s_sq, t + 1)
                v.tensor_reduce(ss[:], sq[:].rearrange("p (h d) -> p h d", d=DH), AX_X, ALU.add).then_inc(s_ss, 1)
                wait(dve, s_ss, 2 * t + 1)
                v.scalar_tensor_tensor(out=z[:], in0=ss[:], scalar=1.0 / SCALE, in1=clamp[:],
                                       op0=ALU.mult, op1=ALU.max).then_inc(s_ss, 1)

            def normed_qk(t):
                wait(dve, s_rq, t + 1)
                wait(dve, s_kvcp, t + 1)
                wait(dve, s_lo, t)
                v.tensor_tensor(qn[:].rearrange("p (h d) -> p h d", d=DH),
                                qkv[:, 0:NQK * DH].rearrange("p (h d) -> p h d", d=DH),
                                rq[:].rearrange("p (h o) -> p h o", o=1).broadcast_to([P, NQK, DH]),
                                ALU.mult).then_inc(s_qn, 1)

            def low_parts(t):
                qn3 = qn[:].rearrange("p (h d) -> p h d", d=DH)
                wait(dve, s_hi, t + 1)
                v.tensor_tensor(qs[:, 0:H, DH:2 * DH], qn3[:, 0:H, :], qs[:, 0:H, 0:DH], ALU.subtract)
                v.tensor_tensor(qs[:, H + 1, 0:DH], qn3[:, H, :], qs[:, H, 0:DH], ALU.subtract)
                v.tensor_tensor(qs[:, H + 1, DH:2 * DH], qn3[:, H, :], qs[:, H, 0:DH],
                                ALU.subtract).then_inc(s_lo, 1)

            def low_v(t, m):
                wait(dve, s_vhi, t + 1)
                v.tensor_tensor(v_next[:, m, DH:2 * DH], qkv[:, NQK * DH:(NQK + 1) * DH],
                                v_next[:, m, 0:DH], ALU.subtract).then_inc(s_vst, 1)

            def k_move(bn, j):
                wait(dve, s_kst, TB * bn + 2 * j + 2)
                wait(dve, s_scores, (bn - 1) * TB * NS + TB * NS - 3 + j)
                v.tensor_copy(k_cur[:, :, 2 * j * P:(2 * j + 2) * P],
                              k_next[:, :, 2 * j * P:(2 * j + 2) * P]).then_inc(s_kcur, 1)

            def q_move(bn, half):
                wait(dve, s_qst, TB * bn + HT * (half + 1))
                wait(dve, s_scores, (bn - 1) * TB * NS + 4 * NS * (half + 1))
                v.tensor_copy(q_cur[:, half, :, :], q_next[:]).then_inc(s_qcur, 1)

            stats_1(0, 0, -1)
            norm_1(0, 0, -1)
            dve.wait_ge(s_modcp, 1)
            v.tensor_scalar_add(rows_a[:, 1, :], mod[:, 0, 1, :], 1.0)
            v.tensor_copy(rows_a[:, 0, :], mod[:, 0, 0, :]).then_inc(s_rowa, 1)
            stats_2(0, 0, -1, 0)
            norm_2(0, 0, -1, 0)
            stats_1(1, 1, -1)
            norm_1(1, 1, -1)
            stats_2(1, 1, -1, 0)
            dve.wait_ge(s_modcp, NB)
            v.tensor_scalar_add(mod[:, :, 1, :], mod[:, :, 1, :], 1.0).then_inc(s_mod1, 1)
            norm_2(1, 1, -1, 0)
            for t in range(TB):
                ahead = t + 2 <= TB
                if ahead:
                    stats_1(t + 2, t + 2, -1)
                    norm_1(t + 2, t + 2, -1)
                if t + 2 == TB:
                    wait(dve, s_ha, 2 * TB)
                    wait(dve, s_mod1, 1)
                    v.tensor_scalar(rows_a[:], rows_of(1, 0, 2), 1.0, None, ALU.mult).then_inc(s_rowa, 1)
                squared_norms(t)
                if ahead:
                    stats_2(t + 2, t + 2, -1, 0)
                low_v(t, t)
                if t >= 1:
                    low_parts(t - 1)
                if t < 6:
                    gate_step(t)
                normed_qk(t)
                if ahead:
                    norm_2(t + 2, t + 2, -1, 0)
                if t == HT + 1:
                    q_move(0, 0)
            low_parts(TB - 1)
            for j in range(3):
                k_move(0, j)
            dve.wait_ge(s_modr, 1)

            def macro(b, m):
                M = b * TB + m
                ta, t, r, rp = M + 9, M + 8, M - 4, M - 5
                for s in range(NS):
                    X = M * NS + s
                    if m == 0 and s < 4 and known(b, 0, NB):
                        wait(dve, s_vst, TB * b + 2 * s + 2)
                        wait(dve, s_pv, (b - 1) * TB * NS + TB * NS - 3 + s)
                        wait(dve, s_ones, 2)
                        v.tensor_copy(v_cur[:, 2 * s:2 * s + 2, :], v_next[:, 2 * s:2 * s + 2, :]).then_inc(s_vcur, 1)
                    if known(X, 0, NT * NS):
                        wait(dve, s_exp, X + 1)
                        wait(dve, s_pv, X - RING + 1)
                        pr = probs[:, s % RING, :]
                        hi = pr.bitcast(BF16).rearrange("p (n two) -> p n two", two=2)[:, :, 1]
                        v.tensor_tensor(rest[:, s % RING, :], pr, hi, ALU.subtract).then_inc(s_rest, 1)

                    if m == TB - 1 and s in (5, 6, 7) and known(b + 1, 0, NB):
                        k_move(b + 1, s - 5)
                    if m == 0 and s == 0 and known(b, 0, NB):
                        k_move(b, 3)
                    if m == 0 and s == 1 and known(b, 0, NB):
                        q_move(b, 1)
                    if m == 4 and s == 2 and known(b + 1, 0, NB):
                        q_move(b + 1, 0)

                    if s == 0:
                        if m == TB - 1 and known(ta, 0, NT):
                            wait(dve, s_ha, 2 * ta)
                            v.tensor_scalar(rows_a[:], rows_of(b, 0, 2, 2), 1.0, None, ALU.mult).then_inc(s_rowa, 1)
                        if m == 5 and known(rp, 0, NT):
                            wait(dve, s_h2, 2 * rp)
                            v.tensor_scalar(rows_f[:], rows_of(b, 2, 5), 1.0, None, ALU.mult).then_inc(s_rowf, 1)
                        if known(rp, 0, NT):
                            k = (m - 5) % 4
                            wait(dve, s_sc[k], 4 * (rp - k))
                            if m in (5, 6, 7, 0):
                                v.tensor_scalar(pay[:, k, 2 * D:3 * D], gate_of(b - (m == 0)), 1.0, None, ALU.mult)
                            tok = pay[:, k, TOK:TOK + 1]
                            if known(rp, 3, NT):
                                v.tensor_scalar_add(tok, tok, 4.0 * P).then_inc(s_tok, 1)
                            else:
                                v.tensor_scalar_add(tick[:], power[:, 0:1], 1.0).then_inc(s_tok, 1)
                        if cols(ta, rp):
                            stats_1(M + 9, ta, rp)
                    if s == 1 and cols(ta, rp):
                        norm_1(M + 9, ta, rp)
                    if s in (1, 5):
                        U = 2 * M - 1 if s == 1 else 2 * M
                        if known(M - (s == 1), 0, NT):
                            par = 1 if s == 1 else 0
                            wait(dve, s_ocp, U + 1)
                            wait(dve, s_onorm, U - 1)
                            v.reciprocal(o_rin[:, par, :], o_raw[:, par, :, 2 * DH]).then_inc(s_orin, 1)
                    if s == 3 and cols(ta, rp):
                        stats_2(M + 9, ta, rp, m)
                    if s == 4 and cols(ta, rp):
                        norm_2(M + 9, ta, rp, m)
                    q = M - 6
                    if s == 2 and known(q, 0, NT):
                        wait(dve, s_lg, q + 1)
                        wait(dve, s_pl, 3 * q)
                        v.tensor_reduce(lg_max[:], lg[:], AX_X, ALU.max).then_inc(s_rt, 1)
                        wait(dve, s_rt, 4 * q + 1)
                        v.scalar_tensor_tensor(out=lg_eq[:], in0=lg[:], scalar=lg_max[:, 0:1], in1=first_pref[:],
                                               op0=ALU.is_ge, op1=ALU.mult).then_inc(s_rt, 1)
                        wait(dve, s_rt, 4 * q + 2)
                        v.tensor_reduce(eq_max[:], lg_eq[:], AX_X, ALU.max).then_inc(s_rt, 1)
                        wait(dve, s_rt, 4 * q + 3)
                        wait(dve, s_cnt, q)
                        v.tensor_scalar(chosen[:], lg_eq[:], eq_max[:, 0:1], None, ALU.is_equal)
                        v.tensor_scalar(chosen16[:], lg_eq[:], eq_max[:, 0:1], None, ALU.is_equal).then_inc(s_rt, 1)
                    if s == 4 and known(t, 0, NT):
                        squared_norms(t)
                    if s == 4 and known(q, 0, NT):
                        wait(dve, s_jr, q + 1)
                        v.tensor_tensor(place[:], ps_m0[:, 0:E], e_base[:], ALU.add).then_inc(s_pl, 1)
                        v.tensor_tensor(counted[:], counted[:], chosen16[:], ALU.add).then_inc(s_cnt, 1)
                        wait(dve, s_pl, 3 * q + 1)
                        v.tensor_tensor_reduce(place_c[:], place[:], chosen[:], 1.0, 0.0, ALU.mult, ALU.add,
                                               dest[:]).then_inc(s_pl, 1)
                        wait(dve, s_pl, 3 * q + 2)
                        k = (m - 6) % 4
                        wait(dve, s_sc[k], 4 * (q - k))
                        v.tensor_copy(dest_i[:, k, :], dest[:]).then_inc(s_pl, 1)
                    if known(t, 0, NT):
                        if s == 5:
                            low_v(t, m)
                        if s == 6:
                            normed_qk(t)
                        if s == 7:
                            low_parts(t)

            sweep(dve, macro)

            n = [0]

            def step(ins):
                n[0] += 1
                ins.then_inc(f_map, 1)
                dve.wait_ge(f_map, n[0])
            dve.wait_ge(f_tot, 1)
            step(v.tensor_copy(total[:], ps_m1[:, 0:E]))
            step(v.tensor_tensor(fill_i[:], total[:], e_base[:], ALU.add))
            assert n[0] == FILL_STEPS
            step(v.tensor_scalar_add(total_i[:], total[:], float(P - 1)))
            step(v.tensor_scalar(total_i[:], total_i[:], 7, None, ALU.logical_shift_right))
            step(v.tensor_copy(nblk[:], total_i[:]))
            step(v.memset(start[:, 0:1], 0.0))
            for e in range(E):
                step(v.tensor_tensor(start[:, e + 1:e + 2], start[:, e:e + 1], nblk[:, e:e + 1], ALU.add))
            step(v.tensor_scalar(jump[:], nblk[:], -float(P), float(CAP), ALU.mult, ALU.add))
            over_e = blk[:].rearrange("p (o j) -> p o j", o=1).broadcast_to([P, E, NBLK])

            def over_j(ap):
                return ap.rearrange("p (e o) -> p e o", o=1).broadcast_to([P, E, NBLK])
            step(v.tensor_tensor(past, over_e, over_j(start[:, 1:E + 1]), ALU.is_ge))
            step(v.tensor_tensor(past_j, past, over_j(jump[:]), ALU.mult))
            step(v.tensor_reduce(exp_f[:], past.rearrange("p e j -> p j e"), AX_X, ALU.add))
            step(v.tensor_reduce(row_f[:], past_j.rearrange("p e j -> p j e"), AX_X, ALU.add))
            step(v.scalar_tensor_tensor(out=row_f[:], in0=blk[:], scalar=float(P), in1=row_f[:],
                                        op0=ALU.mult, op1=ALU.add))
            step(v.tensor_scalar(exp_f[:], exp_f[:], float(E - 1), None, ALU.min))
            step(v.tensor_tensor(exp_f[:], exp_f[:], digit[:].rearrange("p j k -> p (j k)"), ALU.mult))
            step(v.tensor_reduce(word_f[:], exp_f[:].rearrange("p (w k) -> p w k", k=WORD), AX_X, ALU.add))
            step(v.tensor_copy(exp_tab[:], word_f[:]))
            step(v.tensor_scalar(row_tab[:], row_f[:], float(E * CAP), None, ALU.min))
            assert n[0] == MAP_STEPS, n[0]

            def split_hT(j, k):
                wait(dve, f_hT, j + 1)
                wait(dve, f_F, j - 1)
                v.tensor_tensor(hT_lo[:, k % 2, :], hT[:, k % 2, :], top(hT[:, k % 2, :]), ALU.subtract
                                ).then_inc(f_hL, 1)

            def split_act(j, k):
                wait(dve, f_sq, j + 1)
                wait(dve, f_D, j - 1)
                v.tensor_tensor(act2_lo[:, k % 2, :], act2[:, k % 2, :], top(act2[:, k % 2, :]), ALU.subtract
                                ).then_inc(f_gL, 1)

            def finish(j, k):
                wait(dve, f_sc[k % 4], 4 * (j - k % 4))
                wait(dve, f_ld[k], 16 // BR * (j - k) + 16)
                v.tensor_copy(tok_i[:, k % 4, :], b_in[:, k, TOK:TOK + 1])
                wait(dve, f_D, j + 1)
                bank = (ps_m0, ps_m1)[k % 2]
                v.tensor_reduce(y_s[:, k % 2, :], bank[:, 0:2 * D].rearrange("p (two d) -> p d two", two=2),
                                AX_X, ALU.add).then_inc(f_ys, 1)
                wait(dve, f_ys, j + 1)
                v.tensor_tensor(y_g[:, k % 2, :], y_s[:, k % 2, :], b_in[:, k, 2 * D:3 * D], ALU.mult).then_inc(f_yg, 1)
                wait(dve, f_yg, j + 1)
                v.tensor_tensor(y_fin[:, k % 4, :], y_g[:, k % 2, :], b_in[:, k, D:2 * D], ALU.add).then_inc(f_yf, 1)

            run_blocks(dve, (split_hT, 3), (finish, 0), (split_act, UP_AHEAD))

        @block.tensor
        def _(pe):
            te = nc.tensor
            pe.wait_ge(s_silub, 1)
            pe.wait_ge(s_wm, 16)
            for b in range(NB):
                wait(pe, s_modcp, b - 1)
                te.matmul(ps_s[:, b % 2, 0, 0:3 * D], silu_b[:, b, :], wmod_sb[:, 0:3 * D], start=True, stop=True)
                te.matmul(ps_s[:, b % 2, 1, 0:3 * D], silu_b[:, b, :], wmod_sb[:, 3 * D:6 * D],
                          start=True, stop=True).then_inc(s_modmm, 1)
            pe.wait_ge(s_const, 1)
            pe.wait_ge(s_w, 16 * 6)
            te.transpose(ps_m0[:, 0:E], router_sb[:], ident[0:E, 0:E]).then_inc(s_rT, 1)
            pe.wait_ge(s_modcp, NB + 1)

            def turn_q(dst):
                for h in range(H):
                    last = te.transpose(dst[:, h * P:(h + 1) * P], qs[:, h, :], ident16[:])
                last.then_inc(s_jqT, 1)

            def turn_k(dst):
                for j in range(2):
                    last = te.transpose(dst[:, j * P:(j + 1) * P], qs[:, H + j, :], ident16[:])
                last.then_inc(s_jkT, 1)

            def scores(b, m, s):
                X = (b * TB + m) * NS + s
                s2 = s + LOOK
                m2 = m + s2 // NS
                s2 %= NS
                bo, m2 = m2 // TB, m2 % TB
                half, h, jj = m2 // 4, 2 * (m2 % 4) + s2 // 4, s2 % 4
                if m2 % 4 == 0 and s2 == 0:
                    wait(pe, s_qcur, 2 * (b + bo) + half + 1)
                if m2 == 0 and s2 < 4:
                    wait(pe, s_kcur, 4 * (b + bo) + jj + 1)
                wait(pe, s_exp, X + LOOK - 1)
                for jc in range(2):
                    for part in range(2):
                        ch = 2 * jj + jc
                        last = te.matmul(ps_s[:, s2 % 2, jc, :], k_cur[:, part, ch * P:(ch + 1) * P],
                                         q_cur[:, half, h, :], start=(part == 0), stop=(part == 1))
                last.then_inc(s_scores, 1)

            def project(t):
                pe.wait_ge(s_xh, t + 1)
                wait(pe, s_qcp, t)
                te.transpose(ps_m0[:, 0:P], xhat[:], ident[:]).then_inc(s_ja, 1)
                pe.wait_ge(s_xnT, t + 1)
                te.matmul(ps_m0[:, 0:INNER], xnT[:], wq_sb[:], start=True, stop=True).then_inc(s_jq, 1)
                wait(pe, s_kvcp, t)
                te.matmul(ps_m1[:, 0:2 * DH], xnT[:], wkv_sb[:], start=True, stop=True).then_inc(s_jkv, 1)

            project(0)
            for t in range(TB):
                if t + 1 < TB:
                    project(t + 1)
                if t >= 1:
                    pe.wait_ge(s_lo, t)
                    wait(pe, s_qst, t - 1)
                    turn_q(ps_o0h)
                    wait(pe, s_kst, t - 1)
                    turn_k(ps_o1h)
                wait(pe, s_pw, 16)
                wait(pe, s_pjc, t - 1)
                for j in range(HC):
                    last = te.transpose(ps_s[:, t % 2, 0, j * P:(j + 1) * P], pj_in[:, t, j * P:(j + 1) * P], ident[:])
                last.then_inc(s_pj, 1)
            pe.wait_ge(s_pjc, E)
            for s in range(LOOK):
                scores(-1, TB - 1, NS - LOOK + s)

            def macro(b, m):
                M = b * TB + m
                t, tp, r, rp = M + 8, M + 7, M - 4, M - 5
                for s in range(NS):
                    X = M * NS + s
                    if s == 0 and known(tp, 0, NT):
                        wait(pe, s_lo, tp + 1)
                        bank_free(pe, M1_JOBS, b, m, s)
                        turn_k(ps_m1h)
                        bank_free(pe, M0_JOBS, b, m, s)
                        turn_q(ps_m0h)
                    if s == 1 and known(t, 0, NT):
                        wait(pe, s_xh, t + 1)
                        bank_free(pe, M0_JOBS, b, m, s)
                        te.transpose(ps_m0[:, 0:P], xhat[:], ident[:]).then_inc(s_ja, 1)
                    if s == 3 and known(t, 0, NT):
                        wait(pe, s_xnT, t + 1)
                        bank_free(pe, M0_JOBS, b, m, s)
                        te.matmul(ps_m0[:, 0:INNER], xnT[:], wq_sb[:], start=True, stop=True).then_inc(s_jq, 1)
                        bank_free(pe, M1_JOBS, b, m, s)
                        te.matmul(ps_m1[:, 0:2 * DH], xnT[:], wkv_sb[:], start=True, stop=True).then_inc(s_jkv, 1)
                    if s == 4 and known(r, 0, NT):
                        wait(pe, s_onorm, 8 * (r // 4 + 1) if isinstance(b, int)
                             else 16 * b + 8 * ((m - 4) // 4 + 1))
                        bank_free(pe, M1_JOBS, b, m, s)
                        g_par = ((m - 4) // 4) % 2
                        for j in range(INNER // P):
                            last = te.transpose(ps_m1[:, j * P:(j + 1) * P], o_all[:, g_par, (m - 4) % 4, j * P:(j + 1) * P],
                                                ident[:])
                        last.then_inc(s_jo, 1)
                    if s == 4 and known(M - 6, 0, NT):
                        wait(pe, s_rt, 4 * (M - 5))
                        wait(pe, s_cnt, M - 6)
                        bank_free(pe, M0_JOBS, b, m, s)
                        te.matmul(ps_m0[:, 0:E], below[:], chosen16[:], start=True, stop=False)
                        te.matmul(ps_m0[:, 0:E], ones16[:], counted[:], start=False, stop=True).then_inc(s_jr, 1)
                    if s == y_slot(b) and known(r, 0, NT):
                        wait(pe, s_oT, r + 1)
                        if after_last(b):
                            wait(pe, s_exp, NT * NS)
                            wait(pe, s_y, r)
                        else:
                            bank_free(pe, M0_JOBS, b, m, s)
                        for j in range(INNER // P):
                            last = te.matmul(y_bank(b), oT[:, j, :], wout_sb[:, j, :], start=(j == 0),
                                             stop=(j == INNER // P - 1))
                        last.then_inc(s_jy, 1)
                    if s == 6 and known(rp, 0, NT):
                        wait(pe, s_h2, 2 * (rp + 1))
                        bank_free(pe, M1_JOBS, b, m, s)
                        te.transpose(ps_m1[:, 0:P], pay[:, (m - 5) % 4, 0:D], ident[:]).then_inc(s_jh, 1)
                    if s == 7 and known(rp, 0, NT):
                        wait(pe, s_h2T, rp + 1)
                        bank_free(pe, M0_JOBS, b, m, s)
                        te.matmul(ps_m0[:, 0:E], h2T[:], routerT[:], start=True, stop=True).then_inc(s_jl, 1)

                    if known(X + LOOK, 0, NT * NS):
                        scores(b, m, s)
                    if known(X - 1, 0, NT * NS):
                        s1 = (s - 1) % NS
                        m1 = (m - (s == 0)) % TB
                        jj = s1 % 4
                        if m1 == 0 and s1 < 4:
                            wait(pe, s_vcur, 4 * b + jj + 1)
                        if jj == 0:
                            wait(pe, s_ocp, 2 * M + s1 // 4)
                        wait(pe, s_rest, X)
                        for jc in range(2):
                            for it in range(HT):
                                o = ps_o[:, it // 2, (it % 2) * VC:(it % 2 + 1) * VC]
                                vv = v_cur[:, 2 * jj + jc, 0:VC]
                                cols_ = slice(jc * HALF + it * P, jc * HALF + (it + 1) * P)
                                te.matmul(o, top(probs[:, s1 % RING, :])[:, cols_], vv,
                                          start=(jj == 0 and jc == 0 and it % 2 == 0),
                                          stop=False, skip_group_check=True)
                                last = te.matmul(o, rest[:, s1 % RING, cols_], vv, start=False,
                                                 stop=(jj == 3 and jc == 1), skip_group_check=True)
                        last.then_inc(s_pv, 1)

            sweep(pe, macro)

            pe.wait_ge(s_cnt, NT)
            bank_free(pe, M1_JOBS, NB + 1, 0, 0)
            te.matmul(ps_m1[:, 0:E], ones16[:], counted[:], start=True, stop=True).then_inc(f_tot, 1)
            pe.wait_ge(f_map, MAP_STEPS)
            pe.wait_ge(s_wlo, 2 * E)

            experts = []

            def load_experts(j):
                n = BR // WORD if isinstance(j, int) and j > 0 else BR // WORD + 1
                w = j // WORD if isinstance(j, int) else (j // BR) * (BR // WORD)
                tab = exp_tab[0:1, w:w + n] if isinstance(j, int) else exp_tab[0:1, bass.ds(w, n)]
                words = nc.values_load_multi_w_load_instructions(
                    tab, engines=[mybir.EngineType.PE], min_val=0, max_val=E ** WORD - 1)[1]
                experts[:] = [pe.snap((words[k // WORD] // E ** (k % WORD)) % E * HID)
                              for k in range(min(n * WORD, BR + UP_AHEAD))]

            fc_flat = fc_sb[:].rearrange("p e h -> p (e h)")
            fc_top, fc_low = top(fc_flat), fc_lo[:].rearrange("p e h -> p (e h)")
            pj_flat = pj_hl[:].rearrange("p e j two d -> p (e j two d)")

            def turn_rows(j, k):
                wait(pe, f_ld[k], 16 // BR * (j - k) + 16)
                wait(pe, f_hT, j - 1)
                te.transpose(ps_o[:, k % 2, 0:P], b_in[:, k, 0:D], ident[:]).then_inc(f_T, 1)

            def up(j, k):
                e = experts[k + BR if k < UP_AHEAD and j is not k else k]
                wait(pe, f_hL, j + 1)
                wait(pe, f_rl, j - 1)
                for c4 in range(HC):
                    for n, w in enumerate((fc_top, fc_low)):
                        wc = w[:, bass.ds(e + c4 * P, P)]
                        te.matmul(ps_s[:, 0, k % 2, c4 * P:(c4 + 1) * P], wc, top(hT[:, k % 2, :]),
                                  start=(n == 0), stop=False)
                        last = te.matmul(ps_s[:, 0, k % 2, c4 * P:(c4 + 1) * P], wc, hT_lo[:, k % 2, :],
                                         start=False, stop=(n == 1))
                last.then_inc(f_F, 1)

            def down(j, k):
                e = experts[k]
                wait(pe, f_gL, j + 1)
                wait(pe, f_ys, j - 1)
                bank = (ps_m0, ps_m1)[k % 2]
                for c4 in range(HC):
                    cols = slice(c4 * P, (c4 + 1) * P)
                    w = pj_flat[:, bass.ds(2 * e + c4 * 2 * D, 2 * D)]
                    for n, g2 in enumerate((top(act2[:, k % 2, :])[:, cols], act2_lo[:, k % 2, cols])):
                        last = te.matmul(bank[:, 0:2 * D], g2, w, start=(c4 == 0 and n == 0),
                                         stop=(c4 == HC - 1 and n == 1))
                last.then_inc(f_D, 1)

            run_blocks(pe, (turn_rows, 3), (up, UP_AHEAD), (down, 0), group=load_experts)


_INS = ['L0_attn_x', 'L0_attn_norm_g', 'L0_attn_Wq', 'L0_attn_Wkv', 'L0_attn_Wout', 'L0_attn_out_norm_g',
        'L0_ffn_router_w', 'L0_ffn_expert_fc', 'L0_ffn_expert_proj', 'L0_c', 'L0_wmod']


def kernel(**inputs):
    import numpy as _np
    import concourse.bacc as _bacc
    from concourse import mybir as _mybir
    from concourse.bass_utils import run_bass_kernel_spmd as _run

    nc = _bacc.Bacc("TRN2", target_bir_lowering=False, num_devices=1)
    arrays, args = {}, []
    for name in _INS:
        a = _np.asarray(inputs[name])
        a = _np.ascontiguousarray(a.T if name == 'L0_c' else a)
        arrays[f"in_{name}_dram"] = a
        args.append(nc.dram_tensor(f"in_{name}_dram", a.shape, _mybir.dt.from_np(a.dtype), kind="ExternalInput").ap())
    shape = tuple(inputs['L0_attn_x'].shape)
    args.append(nc.dram_tensor("out_0_dram", shape, F32, kind="ExternalOutput").ap())
    build(nc, *args)
    r = _run(nc, [arrays], core_ids=[0])
    return r.results[0]["out_0_dram"]
```
